# Optimizing a Trainium2 kernel written in Bass

```python
import numpy as np
import jax
import jax.numpy as jnp

def _softmax(x, axis=-1):
    return jax.nn.softmax(x, axis=axis)

def _gelu(x):
    return jax.nn.gelu(x, approximate=True)

def _silu(x):
    return jax.nn.silu(x)

def _sigmoid(x):
    return jax.nn.sigmoid(x)

def _layernorm(x, axis=-1, eps=1e-05):
    m = jnp.mean(x, axis=axis, keepdims=True)
    v = jnp.var(x, axis=axis, keepdims=True)
    return (x - m) / jnp.sqrt(v + eps)

def _scatter_add(tgt, idx, src, axis=0):
    return tgt.at[idx].add(src)

def _segment_sum(src, seg, n):
    return jax.ops.segment_sum(src, seg, n)
kernel_name = 'mk_xattn_ffn_d1_seqx_r4_4d04ca'

def setup_inputs(seed: int=0):
    np.random.seed(seed)
    _w = jnp.asarray

    def _rec_inputs():
        import jax
        import jax.numpy as jnp
        _rk = jax.random.key(seed)
        x = -0.0002928 + 1 * jax.random.normal(jax.random.fold_in(_rk, 1), (8, 512, 256), jnp.float32)
        _lenS = 512 - jax.random.randint(jax.random.fold_in(_rk, 7), (8,), 0, max(1, 512 // 4) + 1, jnp.int32)
        _lenS2 = 512 - jax.random.randint(jax.random.fold_in(_rk, 8), (8,), 0, max(1, 512 // 4) + 1, jnp.int32)
        _ctx_1024P = jax.random.normal(jax.random.fold_in(_rk, 11), (8, 16, 256), jnp.float32)
        _ctx_1024c = jax.random.dirichlet(jax.random.fold_in(_rk, 511), 0.3 * jnp.ones((16,), jnp.float32), (8, 512))
        _ctx_1024t = jnp.einsum('bsk,bkd->bsd', _ctx_1024c, _ctx_1024P)
        _ctx_1024t = _ctx_1024t * jax.lax.rsqrt(jnp.mean(jnp.square(_ctx_1024t)) + 1e-12) * 0.953939
        ctx_1024 = -1.39393e-06 + 0.999914 * (_ctx_1024t + 0.3 * jax.random.normal(jax.random.fold_in(_rk, 611), (8, 512, 256), jnp.float32))
        return (x, ctx_1024)
    x, ctx_1024 = _rec_inputs()

    def _L0_xattn_setup():
        import jax, jax.numpy as jnp
        import numpy as np
        B, T, D, H = (2, 512, 256, 16)
        DH = D // H
        key = jax.random.key(seed)
        ks = jax.random.split(key, 11)
        s = 1.0 / np.sqrt(D)
        return {'q': jax.random.normal(ks[0], (B, T, D), jnp.float32), 'k': jax.random.normal(ks[1], (B, T, D), jnp.float32), 'v': jax.random.normal(ks[2], (B, T, D), jnp.float32), 'wq_w': jax.random.normal(ks[3], (D, D), jnp.float32) * s, 'wq_b': jnp.zeros((D,), jnp.float32), 'wk_w': jax.random.normal(ks[4], (D, D), jnp.float32) * s, 'wk_b': jnp.zeros((D,), jnp.float32), 'wv_w': jax.random.normal(ks[5], (D, D), jnp.float32) * s, 'wv_b': jnp.zeros((D,), jnp.float32), 'wo_w': jax.random.normal(ks[6], (D, D), jnp.float32) * s, 'wo_b': jnp.zeros((D,), jnp.float32)}
    _L0_xattn_all = _L0_xattn_setup()
    _L0_xattn_in = {k: v for k, v in _L0_xattn_all.items() if k in ('wq_w', 'wq_b', 'wk_w', 'wk_b', 'wv_w', 'wv_b', 'wo_w', 'wo_b')}
    del _L0_xattn_all

    def _L0_ffn_setup():
        import jax, jax.numpy as jnp
        import numpy as np
        B, S, D, H, E = (2, 512, 256, 1024, 8)
        key = jax.random.key(seed)
        k0, k1, k2, k3 = jax.random.split(key, 4)
        x = jax.random.normal(k0, (B, S, D), dtype=jnp.float32)
        router_w = jax.random.normal(k1, (E, D), dtype=jnp.float32) * 0.02
        w1 = jax.random.normal(k2, (E, D, H), dtype=jnp.float32) * 0.02
        w2 = jax.random.normal(k3, (E, H, D), dtype=jnp.float32) * 0.02
        return {'x': x, 'router_w': router_w, 'w1': w1, 'w2': w2}
    _L0_ffn_all = _L0_ffn_setup()
    _L0_ffn_in = {k: v for k, v in _L0_ffn_all.items() if k in ('router_w', 'w1', 'w2')}
    del _L0_ffn_all
    return {'x': x, 'ctx_1024': ctx_1024, 'L0_xattn_wq_w': _L0_xattn_in['wq_w'], 'L0_xattn_wq_b': _L0_xattn_in['wq_b'], 'L0_xattn_wk_w': _L0_xattn_in['wk_w'], 'L0_xattn_wk_b': _L0_xattn_in['wk_b'], 'L0_xattn_wv_w': _L0_xattn_in['wv_w'], 'L0_xattn_wv_b': _L0_xattn_in['wv_b'], 'L0_xattn_wo_w': _L0_xattn_in['wo_w'], 'L0_xattn_wo_b': _L0_xattn_in['wo_b'], 'L0_ffn_router_w': _L0_ffn_in['router_w'], 'L0_ffn_w1': _L0_ffn_in['w1'], 'L0_ffn_w2': _L0_ffn_in['w2']}

def reference(x, ctx_1024, L0_xattn_wq_w, L0_xattn_wq_b, L0_xattn_wk_w, L0_xattn_wk_b, L0_xattn_wv_w, L0_xattn_wv_b, L0_xattn_wo_w, L0_xattn_wo_b, L0_ffn_router_w, L0_ffn_w1, L0_ffn_w2):
    import jax
    import jax.numpy as jnp

    def _L0_xattn_ref(q, k, v, wq_w, wq_b, wk_w, wk_b, wv_w, wv_b, wo_w, wo_b):
        import jax, jax.numpy as jnp
        import numpy as np
        B, T, D, H = (2, 512, 256, 16)
        DH = D // H
        b, t, d = q.shape
        wq = (q @ wq_w.T + wq_b).reshape(b, t, H, DH)
        wk = (k @ wk_w.T + wk_b).reshape(b, t, H, DH)
        wv = (v @ wv_w.T + wv_b).reshape(b, t, H, DH)
        scores = jnp.einsum('bthd,bshd->bhts', wq, wk) / jnp.sqrt(jnp.float32(DH))
        probs = jax.nn.softmax(scores, axis=-1)
        attn = jnp.einsum('bhts,bshd->bthd', probs, wv)
        attn = attn.reshape(b, t, d)
        return attn @ wo_w.T + wo_b

    def _L0_ffn_ref(x, router_w, w1, w2):
        import jax, jax.numpy as jnp
        import numpy as np
        B, S, D, H, E = (2, 512, 256, 1024, 8)
        b, s, d = x.shape
        e = router_w.shape[0]
        xf = x.reshape(-1, d)
        probs = jax.nn.softmax(xf @ router_w.T, axis=-1)
        topv, topi = jax.lax.top_k(probs, 2)
        topv = topv / (topv.sum(axis=-1, keepdims=True) + 1e-09)
        cw = (jax.nn.one_hot(topi, e, dtype=xf.dtype) * topv[..., None]).sum(axis=1)
        h = jax.nn.gelu(jnp.einsum('td,edh->teh', xf, w1), approximate=False)
        y = jnp.einsum('teh,ehd->ted', h, w2)
        out = jnp.einsum('te,ted->td', cw, y)
        return out.reshape(b, s, d)
    x = x + _L0_xattn_ref(_layernorm(x, axis=-1), ctx_1024, ctx_1024, L0_xattn_wq_w, L0_xattn_wq_b, L0_xattn_wk_w, L0_xattn_wk_b, L0_xattn_wv_w, L0_xattn_wv_b, L0_xattn_wo_w, L0_xattn_wo_b)
    x = x + _L0_ffn_ref(_layernorm(x, axis=-1), L0_ffn_router_w, L0_ffn_w1, L0_ffn_w2)
    return x

_drawn_inputs = setup_inputs


def setup_inputs(seed=0):
    import zlib

    import numpy as np

    out = dict(_drawn_inputs(seed))
    spreads = {'L0_xattn_wq_b': (0.0, 0.397),
     'L0_xattn_wk_b': (0.0, 0.8),
     'L0_xattn_wv_b': (0.0, 0.1),
     'L0_xattn_wo_b': (0.0, 0.1)}
    factors = {}
    for name, (base, spread) in spreads.items():
        noise = np.random.default_rng([zlib.crc32(name.encode()), seed]).standard_normal(out[name].shape)
        drawn = base * np.exp(spread * noise) if base else spread * noise
        out[name] = jnp.asarray(drawn.astype(out[name].dtype))
    for name, factor in factors.items():
        out[name] = (out[name] * factor).astype(out[name].dtype)
    return out
```

```python
from contextlib import ExitStack

import concourse.bass as bass
from concourse import mybir

F32 = mybir.dt.float32
F16 = mybir.dt.float16
BF16 = mybir.dt.bfloat16
I32 = mybir.dt.int32
U32 = mybir.dt.uint32
ALU = mybir.AluOpType
ACT = mybir.ActivationFunctionType
AX = mybir.AxisListType

P = 128
B, T, D = 8, 512, 256
NH, DH = 16, 16
KC = D // P
TT = T // P
E, HID = 8, 1024
HC = HID // P
N = B * T
REGION = N + P
XW = D
W_CW, W_ID, ROWW = XW, XW + E, XW + E + 1
WSC = 256.0
PARTS = 3
RUNS = ((0, 48, 0, 3), (48, 32, 0, 2), (80, 16, 0, 1))
KRUNS = ((0, 48, 0, 3), (48, 32, 1, 3), (80, 16, 2, 3))
ORDER = (2, 3, 0, 1)
KS, KM = 96, 98
STEPS = 16
LEAD = 7
EPS = 1e-5


def build(nc, x, ctxT, wqT, wkT, wvT, woT, bq, bk, bv, bo, rwT, w1, w2, out):
    scr = [nc.dram_tensor(f"scr_{n}", [B, NH, PARTS, DH, T], BF16).ap() for n in "qk"]
    wsp = nc.dram_tensor("wsp", [E, P, 8 * HID], F16).ap()
    rows_d = nc.dram_tensor("rows_d", [E * REGION, ROWW], F32).ap()

    with ExitStack() as ctx:
        def sb(name, shape, dt=F32):
            return ctx.enter_context(nc.sbuf_tensor(name, shape, dt))

        def ps(name, shape, dt=F32):
            return ctx.enter_context(nc.psum_tensor(name, shape, dt))

        def sem(name):
            return ctx.enter_context(nc.semaphore(name))

        ident = sb("ident", [P, P])
        ident16 = sb("ident16", [P, P], F16)
        tri = sb("tri", [P, P], BF16)
        ones = sb("ones", [P, P], BF16)
        iota_e = sb("iota_e", [P, TT, E])
        region = sb("region", [P, TT, E])
        tok_id = sb("tok_id", [P, B * TT], I32)
        pad_row = sb("pad_row", [P, ROWW])
        wq = sb("wq", [P, KC, D])
        wk = sb("wk", [P, KC, D])
        wv = sb("wv", [P, KC, D])
        wo = sb("wo", [P, KC, D])
        rw = sb("rw", [P, KC, E])
        bqk = sb("bqk", [P, 4])
        bvb = sb("bvb", [P, D])
        bob = sb("bob", [P, D])
        xt = sb("xt", [P, TT, D])
        xr = sb("xr", [P, TT, D])
        ct = sb("ct", [P, KC, T])
        xn = sb("xn", [P, TT, D])
        xnT = sb("xnT", [P, KC, T])
        parts = sb("parts", [P, 4, PARTS, T], BF16)
        rest = sb("rest", [P, 2, T])
        qst = sb("qst", [P, 4, 4, T], BF16)
        kst = sb("kst", [P, 4, 4, T], BF16)
        vn = sb("vn", [P, TT, D])
        vaug = sb("vaug", [P, 4, TT, 4, 32])
        pT = sb("pT", [P, 2, 4, T])
        pvs = sb("pvs", [P, T])
        attn = sb("attn", [P, TT, D])
        attnT = sb("attnT", [P, KC, T])
        x1 = sb("x1", [P, TT, D])
        xn2 = sb("xn2", [P, TT, D])
        xn2T = sb("xn2T", [P, KC, T])
        row = sb("row", [P, TT, ROWW])
        row16 = row[:, :, 0:XW].bitcast(F16)
        mx = sb("mx", [P, 2, 4, TT])
        mneg = sb("mneg", [16, 2, P], BF16)
        rec = sb("rec", [P, TT, 4])
        lgT = sb("lgT", [E, T])
        stats = sb("stats", [P, 2, TT, 6])
        mv = sb("mv", [P, 2, TT, 2])
        lnv = sb("lnv", [P, 2, TT])
        nt = sb("nt", [P, 2, 5, TT])
        eps_t = sb("eps_t", [P, 1])
        warm = sb("warm", [P, 1])
        lg = sb("lg", [P, TT, E])
        rt = sb("rt", [P, 14, TT, E])
        sm = sb("sm", [P, 12, TT])
        mask = sb("mask", [P, TT, E], BF16)
        base = sb("base", [P, 2, E])
        slots = sb("slots", [P, 2 * TT])
        slots_u = sb("slots_u", [P, 2 * TT], U32)
        cnt_i = sb("cnt_i", [P, 4, E], I32)
        cnt_f = sb("cnt_f", [P, 3, E])
        tab = sb("tab_tiles", [P, 2, E + 1], I32)
        wst = sb("wst", [P, 4 * HID])
        wsh = sb("wsh", [P, 8 * HID], F16)
        whl = [sb(f"whl{q}", [P, 8 * HID], F16) for q in range(2)]
        hf = xt[:].rearrange("p a b -> p (a b)")
        hh = xnT[:].rearrange("p a b -> p (a b)").bitcast(F16)[:, 0:HID]
        hl = xnT[:].rearrange("p a b -> p (a b)").bitcast(F16)[:, HID:2 * HID]
        xrow = sb("xrow", [P, XW])
        xrow16 = xrow[:].bitcast(F16)
        xT = sb("xT", [P, 4 * P], F16)
        meta_cw = sb("meta_cw", [P, 1])
        meta_id = sb("meta_id", [P, 1], U32)
        ys = sb("ys", [P, D])

        A = ps("A", [P, 4, T])
        Bp = ps("Bp", [P, 2, T])
        PV = ps("PV", [P, T])
        M = ps("M", [P, T])

        names = """consts cin cin_h c_exp x_in xr_in ct_in bn ag lnv_s y0 nw xn_s xnT_ps xnT_sb qk_ps p1 r_s p2 p3
            v_ps v_sb vaug_s a_done red b_done exp pv pve pvt rec_s attn_g attnT_ps attnT_sb o_ps x1_s xb x1_st
            bn2 ag2 lnv2 y02 nw2 xn2_s xh xl xn2T_ps xn2T_sb lgT_ps lgT_sb lg_ps rtc ex mask_s cw_s rank_ps slot
            idw sct maxT neg fin fin2 tabs padd w_in w_s w_h w_l wst_s wprep xrow_in t_ps xT_s s1 gelu hh_s hl_s s2 y_s
            meta scat outinit ponce tail_a tail_b passed""".split()
        S = {k: sem("s_" + k) for k in names}
        st_part = [sem(f"s_st{i}") for i in range(4)]
        qk_in = [sem(f"s_qk{g}") for g in range(4)]
        mrow = [sem(f"s_mrow{g}") for g in range(4)]
        wld = [sem(f"s_wld{q}") for q in range(2)]

        def wait(eng, s, value):
            eng.wait_ge(s, value)
            if not isinstance(value, int):
                eng.sem_inc(S["passed"], 1)

        def tile_row(i, lo, e):
            return nc.s_assert_within((i - lo) * P + e * REGION, 0, E * REGION - P,
                                      skip_runtime_bounds_check_because="an expert has at most N tokens")

        A4 = M[:].rearrange("p (q j r) -> p q j r", q=TT, j=4)
        Mrow = M[:].rearrange("p (a n) -> p a n", a=2)
        XT16 = M[:].bitcast(F16)[:, 0:4 * P]

        block = ctx.enter_context(nc.Block())

        @block.sync
        def _(sp):
            for w, src in ((wq, wqT), (wk, wkT), (wv, wvT), (wo, woT), (rw, rwT)):
                sp.dma_start(w[:], src.rearrange("(c p) n -> p c n", p=P)).then_inc(S["cin"], 16)
            for i, (bias, h) in enumerate(((bq, 0), (bq, 1), (bk, 0), (bk, 1))):
                sp.dma_start(bqk[:, i:i + 1], bias[h * P:h * P + P].rearrange("(p a) -> p a", a=1)).then_inc(S["cin"], 16)
            for t_, bias in ((bvb, bv), (bob, bo)):
                sp.dma_start(t_[:], bias.rearrange("(a n) -> a n", a=1).to_broadcast([P, D])).then_inc(S["cin"], 16)

            def load_x(b):
                sp.dma_start(xt[:], x[bass.ds(b, 1)].rearrange("a (t p) d -> p (a t) d", p=P)).then_inc(S["x_in"], 16)

            def load_ct(b):
                sp.dma_start(ct[:], ctxT[bass.ds(b, 1)].rearrange("a (c p) t -> p (a c) t", p=P)).then_inc(S["ct_in"], 16)

            def store_parts(n, i):
                dst, h = scr[i // 2], i % 2
                for c in range(PARTS):
                    wait(sp, (S["p1"], S["p2"], S["p3"])[c], 4 * n + i + 1)
                    at = c if i < 2 else PARTS - 1 - c
                    sp.dma_start(dst[bass.ds(n, 1), 8 * h:8 * h + 8, at].rearrange("a h d t -> (a h) d t"),
                                 parts[:, i, c, :]).then_inc(st_part[i], 16)

            def load_stack(n, g, first):
                for i in (g // 2, 2 + g // 2):
                    wait(sp, st_part[i], 48 * (n + 1))
                if not first:
                    wait(sp, S["b_done"], 64 * (n - 1) + 16 * (g + 1))
                for st, src, runs in ((qst, scr[0], RUNS), (kst, scr[1], KRUNS)):
                    for r0, nr, c0, c1 in runs:
                        sp.dma_start(st[r0:r0 + nr, g],
                                     src[bass.ds(n, 1), 4 * g:4 * g + 4, c0:c1].rearrange("a h c d t -> (c d) (a h) t")
                                     ).then_inc(qk_in[g], 16)

            def store_x1(t):
                wait(sp, S["x1_s"], 2 * t + 2)
                sp.dma_start(out[bass.ds(t * T, T)].rearrange("(t p) d -> p t d", p=P), x1[:]).then_inc(S["x1_st"], 16)

            def load_xr(t, first):
                if not first:
                    wait(sp, S["x1_s"], 2 * t)
                sp.dma_start(xr[:], x[bass.ds(t, 1)].rearrange("a (t p) d -> p (a t) d", p=P)).then_inc(S["xr_in"], 16)

            def prep(e, first):
                if not first:
                    wait(sp, S["w_l"], 2 * e)
                sp.dma_start(wst[:, 0:2 * HID].rearrange("p (c n) -> p c n", c=KC),
                             w1[bass.ds(e, 1)].rearrange("a (c p) n -> p (a c) n", p=P)).then_inc(S["w_in"], 16)
                sp.dma_start(wst[:, 2 * HID:4 * HID].rearrange("p (c n) -> p c n", c=HC),
                             w2[bass.ds(e, 1)].rearrange("a (c p) n -> p (a c) n", p=P)).then_inc(S["w_in"], 16)

            def prep_out(e):
                wait(sp, S["w_l"], 2 * e + 2)
                sp.dma_start(wsp[bass.ds(e, 1)].rearrange("a p n -> p (a n)"), wsh[:]).then_inc(S["wprep"], 16)

            load_x(0)
            load_ct(0)
            wait(sp, S["xn_s"], TT)
            load_x(1)
            for i in ORDER:
                store_parts(0, i)
            wait(sp, S["v_ps"], 2)
            load_ct(1)
            for g in range(4):
                load_stack(0, g, True)

            def batch(b, first, last):
                n, t = b + 1, b - 1
                if not first:
                    load_stack(b, 3, False)
                    load_xr(t, first=(isinstance(b, int) and b == 1))
                prep(b, first)
                if not last:
                    for i in ORDER:
                        store_parts(n, i)
                    load_stack(n, 0, False)
                    wait(sp, S["xn_s"], TT * (n + 1))
                    load_x((b + 2) % B)
                    wait(sp, S["v_ps"], 2 * (n + 1))
                    load_ct((b + 2) % B)
                if not first:
                    store_x1(t)
                if not last:
                    load_stack(n, 1, False)
                    load_stack(n, 2, False)
                prep_out(b)

            batch(0, True, False)
            batch(1, False, False)
            with sp.Fori(2, B - 1) as b:
                batch(b, False, False)
            batch(B - 1, False, True)
            load_xr(B - 1, False)
            store_x1(B - 1)

            wait(sp, S["sct"], 16 * 2 * TT * B)
            wait(sp, S["tabs"], 1)
            for e in range(E):
                c = sp.value_load(tab[0:1, 1, e:e + 1], min_val=0, max_val=N)
                sp.dma_start(rows_d[bass.ds(c + e * REGION, P)], pad_row[:]).then_inc(S["padd"], 16)
            wait(sp, S["padd"], 16 * E)

            def load_row(i, at):
                wait(sp, S["xT_s"], i + 1)
                sp.dma_start(xrow[:], rows_d[bass.ds(at, P), 0:XW]).then_inc(S["xrow_in"], 16)

            with sp.Fori(0, E) as e:
                lo = sp.value_load(tab[0:1, 0, bass.ds(e, 1)], min_val=0, max_val=71)
                hi = sp.value_load(tab[0:1, 0, bass.ds(e + 1, 1)], min_val=1, max_val=72)
                with sp.Fori(lo, hi) as i:
                    load_row(i, tile_row(i, lo, e))
            last = sp.value_load(tab[0:1, 0, E:E + 1], min_val=8, max_val=72)
            load_row(last, 0)
            wait(sp, S["xrow_in"], last * 16 + 16)
            wait(sp, S["scat"], last * 16 + 16)

        @block.gpsimd
        def _(pool):
            def once(instr, k):
                instr.then_inc(S["ponce"], 1)
                wait(pool, S["ponce"], k)

            once(nc.gpsimd.memset(ident[:], 0.0), 1)
            once(nc.gpsimd.affine_select(out=ident[:], in_=ident[:], compare_op=ALU.not_equal, fill=1.0, base=0,
                                         pattern=[[-1, P]], channel_multiplier=1), 2)
            once(nc.gpsimd.tensor_copy(ident16[:], ident[:]), 3)
            once(nc.gpsimd.memset(ones[:], 1.0), 4)
            once(nc.gpsimd.affine_select(out=tri[:], in_=ones[:], compare_op=ALU.is_ge, fill=0.0, base=-1,
                                         pattern=[[1, P]], channel_multiplier=-1), 5)
            once(nc.gpsimd.iota(iota_e[:], [[0, TT], [1, E]], base=0, channel_multiplier=0,
                                allow_small_or_imprecise_dtypes=True), 6)
            once(nc.gpsimd.iota(tok_id[:], [[P, B * TT]], base=0, channel_multiplier=1), 7)
            once(nc.gpsimd.memset(pad_row[:], 0.0), 8)
            once(nc.gpsimd.iota(pad_row[:, W_ID:W_ID + 1].bitcast(I32), [[1, 1]], base=N, channel_multiplier=1), 9)
            once(nc.gpsimd.memset(kst[KS:KM], 1.0), 10)
            once(nc.gpsimd.memset(vaug[:], 1.0), 11)
            once(nc.gpsimd.memset(base[:], 0.0), 12)
            once(nc.gpsimd.memset(eps_t[:], EPS), 13)
            once(nc.gpsimd.tensor_scalar(region[:], iota_e[:], float(REGION), None, ALU.mult), 14)
            wait(pool, S["cin"], 16 * 11)
            once(nc.gpsimd.tensor_scalar(wq[:], wq[:], DH ** -0.5, None, ALU.mult), 15)
            nc.gpsimd.tensor_scalar(bqk[:, 0:2], bqk[:, 0:2], DH ** -0.5, None, ALU.mult).then_inc(S["consts"], 1)
            pool.dma_start(out[N:N + P], pad_row[:, 0:D]).then_inc(S["scat"], 16)

            def split(n, i, first):
                k = 4 * n + ORDER.index(i) + 1
                wait(pool, S["r_s"], k)
                if not first:
                    wait(pool, st_part[i], 48 * n)
                nc.gpsimd.tensor_copy(parts[:, i, 1, :], rest[:, i % 2, :]).then_inc(S["p2"], 1)
                wait(pool, S["p2"], k)
                nc.gpsimd.tensor_tensor(parts[:, i, 2, :], rest[:, i % 2, :], parts[:, i, 1, :],
                                        ALU.subtract).then_inc(S["p3"], 1)

            def values(n, g, first):
                wait(pool, S["v_sb"], 2 * n + 2)
                if not first:
                    wait(pool, S["pv"], 16 * (n - 1) + 4 * (g + 1))
                nc.gpsimd.tensor_copy(vaug[:, g, :, :, 0:DH],
                                      vn[:, :, 64 * g:64 * g + 64].rearrange("p t (h d) -> p t h d", h=4)
                                      ).then_inc(S["vaug_s"], 1)

            def expert_weights(e, first):
                if not first:
                    wait(pool, S["wprep"], 16 * e)
                wait(pool, S["w_in"], 32 * (e + 1))
                for k in range(2):
                    a, hi, lo = wst[:, 2 * HID * k:2 * HID * k + 2 * HID], 4 * HID * k, 4 * HID * k + 2 * HID
                    nc.gpsimd.tensor_scalar(a, a, WSC, None, ALU.mult).then_inc(S["w_s"], 1)
                    wait(pool, S["w_s"], 2 * e + k + 1)
                    nc.gpsimd.tensor_copy(wsh[:, hi:hi + 2 * HID], a).then_inc(S["w_h"], 1)
                    wait(pool, S["w_h"], 2 * e + k + 1)
                    nc.gpsimd.tensor_tensor(wsh[:, lo:lo + 2 * HID], a, wsh[:, hi:hi + 2 * HID],
                                            ALU.subtract).then_inc(S["w_l"], 1)

            def residual(t):
                wait(pool, S["xr_in"], 16 * (t + 1))
                nc.gpsimd.tensor_tensor(xr[:], xr[:], bob[:].rearrange("p (a d) -> p a d", a=1).to_broadcast([P, TT, D]),
                                        ALU.add).then_inc(S["xb"], 1)

            def rows(t, first):
                wait(pool, S["xn2_s"], TT * (t + 1))
                if not first:
                    wait(pool, S["sct"], 128 * t)
                nc.gpsimd.tensor_copy(row16[:, :, 0:D], xn2[:]).then_inc(S["xh"], 1)
                wait(pool, S["xh"], t + 1)
                nc.gpsimd.tensor_tensor(row16[:, :, D:2 * D], xn2[:], row16[:, :, 0:D], ALU.subtract).then_inc(S["xl"], 1)
                nc.gpsimd.tensor_copy(row[:, :, W_ID].bitcast(I32), tok_id[:, bass.ds(t * TT, TT)]).then_inc(S["idw"], 1)

            def scatter(t):
                wait(pool, S["slot"], t + 1)
                wait(pool, S["cw_s"], t + 1)
                wait(pool, S["xl"], t + 1)
                wait(pool, S["idw"], t + 1)
                for c in range(2):
                    for tt in range(TT):
                        pool.indirect_dma_start(
                            rows_d, bass.IndirectOffsetOnAxis(slots_u[:, c * TT + tt:c * TT + tt + 1], axis=0),
                            row[:, tt, :], None).then_inc(S["sct"], 16)

            for i in ORDER:
                split(0, i, True)
            for g in range(4):
                values(0, g, True)

            def batch(b, first, last):
                n, t = b + 1, b - 1
                if not first:
                    values(b, 3, False)
                    residual(t)
                if not last:
                    for i in ORDER:
                        split(n, i, False)
                expert_weights(b, first)
                if not first:
                    rows(t, first=(isinstance(b, int) and b == 1))
                if not last:
                    for g in range(3):
                        values(n, g, False)
                if not first:
                    scatter(t)

            batch(0, True, False)
            batch(1, False, False)
            with pool.Fori(2, B - 1) as b:
                batch(b, False, False)
            batch(B - 1, False, True)
            residual(B - 1)
            rows(B - 1, False)
            scatter(B - 1)

            def load_weights(e, q):
                pool.dma_start(whl[q][:], wsp[bass.ds(e, 1)].rearrange("a p n -> p (a n)")).then_inc(wld[q], 16)

            wait(pool, S["wprep"], 16 * E)
            load_weights(0, 0)
            load_weights(1, 1)
            wait(pool, S["padd"], 16 * E)
            wait(pool, S["x1_st"], 16 * B)

            def expert(e, q, first, last=False):
                lo = pool.value_load(tab[0:1, 0, bass.ds(e, 1)], min_val=0, max_val=71)
                hi = pool.value_load(tab[0:1, 0, bass.ds(e + 1, 1)], min_val=1, max_val=72)
                if not first and not last:
                    wait(pool, S["s2"], lo)
                    load_weights(e + 1, 1 - q)
                with pool.Fori(lo, hi) as i:
                    at = tile_row(i, lo, e)
                    wait(pool, S["y_s"], i + 1)
                    pool.dma_start(meta_cw[:], rows_d[bass.ds(at, P), bass.ds(e + W_CW, 1)],
                                   allow_slow_non_contiguous=True).then_inc(S["meta"], 16)
                    wait(pool, S["scat"], 16 * i + 16)
                    pool.dma_start(meta_id[:], rows_d[bass.ds(at, P), W_ID:W_ID + 1].bitcast(U32),
                                   allow_slow_non_contiguous=True).then_inc(S["meta"], 16)
                    wait(pool, S["meta"], 32 * i + 32)
                    wait(pool, S["y_s"], i + 2)
                    pool.indirect_dma_start(out, bass.IndirectOffsetOnAxis(meta_id[:, 0:1], axis=0), ys[:], None,
                                            compute_op=ALU.add).then_inc(S["scat"], 16)

            expert(0, 0, True)
            expert(1, 1, False)
            with pool.Fori(1, E // 2 - 1) as pair:
                expert(2 * pair, 0, False)
                expert(2 * pair + 1, 1, False)
            expert(E - 2, 0, False)
            expert(E - 1, 1, False, True)

        @block.scalar
        def _(act):
            def copy(dst, src):
                return nc.scalar.activation(dst, src, ACT.Copy)

            act.preload_act_table_set("natural_log_exp_and_others")
            act.wait_ge(S["consts"], 1)
            act.wait_ge(S["cin"], 16 * 11)

            def rstd(n, k):
                agg, ls, ys_ = ((S["ag"], S["lnv_s"], S["y0"]), (S["ag2"], S["lnv2"], S["y02"]))[k]
                act.wait_ge(agg, TT * (n + 1))
                nc.scalar.activation(lnv[:, k], mv[:, k, :, 1], ACT.Ln, bias=eps_t[:, 0:1]).then_inc(ls, 1)
                act.wait_ge(ls, n + 1)
                nc.scalar.activation(nt[:, k, 0], lnv[:, k], ACT.Exp, scale=-0.5).then_inc(ys_, 1)

            def xnT_copy(n, c, first):
                act.wait_ge(S["xnT_ps"], 2 * n + c + 1)
                if not first and c == 0:
                    act.wait_ge(S["qk_ps"], 4 * n)
                copy(xnT[:, c], M[:]).then_inc(S["xnT_sb"], 1)

            def part1(n, i, first):
                order = ORDER.index(i)
                act.wait_ge(S["qk_ps"], 4 * n + order + 1)
                if not first:
                    act.wait_ge(st_part[i], 48 * n)
                nc.scalar.activation(parts[:, i, 0, :], M[:], ACT.Identity, bias=bqk[:, i:i + 1]).then_inc(S["p1"], 1)

            def pv_copy(G, first=False):
                act.wait_ge(S["pv"], 4 * G + 4)
                if not first:
                    act.wait_ge(S["pvt"], G)
                copy(pvs[:], PV[:]).then_inc(S["pve"], 1)

            def attnT_copy(t, c, first):
                act.wait_ge(S["attnT_ps"], 2 * t + c + 1)
                if not first and c == 0:
                    act.wait_ge(S["o_ps"], 2 * t)
                copy(attnT[:, c], M[:]).then_inc(S["attnT_sb"], 1)

            def xn2T_copy(t, c, first):
                act.wait_ge(S["xn2T_ps"], 2 * t + c + 1)
                if not first and c == 0:
                    act.wait_ge(S["lgT_ps"], t)
                copy(xn2T[:, c], M[:]).then_inc(S["xn2T_sb"], 1)

            def lgT_copy(t, first):
                act.wait_ge(S["lgT_ps"], t + 1)
                if not first:
                    act.wait_ge(S["lg_ps"], t)
                copy(lgT[:], M[0:E, :]).then_inc(S["lgT_sb"], 1)

            def router_exp(t, first):
                act.wait_ge(S["rtc"], RT * t + 3)
                if not first:
                    act.wait_ge(S["cw_s"], t)
                nc.scalar.activation(rt[:, 1], rt[:, 0], ACT.Exp).then_inc(S["ex"], 1)

            def max_rows(G, g, b):
                act.wait_ge(S["neg"], 2 * G + 2)
                for c in range(2):
                    act.dma_start(qst[KS + c:KS + c + 1, g].rearrange("a h t -> a (h t)"),
                                  mneg[:, c, :]).then_inc(mrow[g], 16)

            def batch(b, first, last):
                n, t = b + 1, b - 1
                second = isinstance(b, int) and b == 1
                for s in range(STEPS):
                    if s % 4 == 1 and not (first and s == 1):
                        pv_copy(4 * b + s // 4 - 1, first=(first and s == 5))
                    if s == 3 and not last:
                        xnT_copy(n, 0, False)
                    if s in (4, 5) and not last:
                        part1(n, (None, None, None, None, 2, 0)[s], False)
                    if s == 6 and not first:
                        attnT_copy(t, 0, second)
                    if s == 12 and not first:
                        xn2T_copy(t, 0, second)
                    if s == 13 and not first:
                        lgT_copy(t, second)
                    for j in range(4):
                        k = (16 * b + s) * 4 + j
                        act.wait_ge(S["b_done"], k + 1)
                        if j == 0 and not (first and s < 2):
                            act.wait_ge(S["pv"], 16 * b + s - 1)
                        nc.scalar.activation(pT[:, s % 2, j, :], Bp[:, j % 2, :], ACT.Exp).then_inc(S["exp"], 1)
                        if s % 4 == 2 and j == 1 and not (last and s == 14):
                            max_rows(4 * b + s // 4 + 1, (s // 4 + 1) % 4, b)
                        if s == 1 and j == 1 and not last:
                            rstd(n, 0)
                        if s == 10 and j == 1 and not first:
                            rstd(t, 1)
                        if s == 14 and j == 3 and not first:
                            router_exp(t, second)
                    if s == 3 and not last:
                        xnT_copy(n, 1, False)
                    if s in (4, 5) and not last:
                        part1(n, (None, None, None, None, 3, 1)[s], False)
                    if s == 6 and not first:
                        attnT_copy(t, 1, second)
                    if s == 12 and not first:
                        xn2T_copy(t, 1, second)

            rstd(0, 0)
            for c in range(KC):
                xnT_copy(0, c, True)
            for i in ORDER:
                part1(0, i, True)
            max_rows(0, 0, 0)

            batch(0, True, False)
            batch(1, False, False)
            with act.Fori(2, B - 1) as b:
                batch(b, False, False)
            batch(B - 1, False, True)
            t = B - 1
            pv_copy(4 * B - 1)
            attnT_copy(t, 0, False)
            attnT_copy(t, 1, False)
            rstd(t, 1)
            xn2T_copy(t, 0, False)
            xn2T_copy(t, 1, False)
            lgT_copy(t, False)
            router_exp(t, False)

            act.wait_ge(S["xn_s"], TT * B)
            nc.scalar.activation(warm[:], eps_t[:, 0:1], ACT.Gelu).then_inc(S["gelu"], 2)
            act.wait_ge(S["tabs"], 1)
            last = act.value_load(tab[0:1, 0, E:E + 1], min_val=8, max_val=72)
            with act.Fori(0, last) as i:
                for k in range(2):
                    act.wait_ge(S["s1"], 2 * i + k + 1)
                    act.wait_ge(S["hl_s"], 2 * i + k + 1)
                    nc.scalar.activation(hf[:, T * k:T * k + T], A[:, k, :], ACT.Gelu,
                                         scale=1.0 / WSC).then_inc(S["gelu"], 1)

        @block.vector
        def _(dve):
            v = nc.vector

            def stats_of(src, n, k, tt, wait):
                if wait is not None:
                    dve.wait_ge(*wait)
                v.bn_stats(stats[:, k, tt], src[:, tt]).then_inc(S[("bn", "bn2")[k]], 1)

            def aggregate(n, k):
                for tt in range(TT):
                    wait(dve, S[("bn", "bn2")[k]], TT * n + tt + 1)
                    v.bn_aggr(mv[:, k, tt], stats[:, k, tt]).then_inc(S[("ag", "ag2")[k]], 1)

            def newton(n, k, step):
                y, a, b_, c_, r = (nt[:, k, m] for m in range(5))
                nw = S[("nw", "nw2")[k]]
                if step == 0:
                    dve.wait_ge(S[("y0", "y02")[k]], n + 1)
                    v.tensor_tensor(a, y, y, ALU.mult).then_inc(nw, 1)
                    return
                dve.wait_ge(nw, 4 * n + step)
                if step == 1:
                    v.scalar_tensor_tensor(b_, mv[:, k, :, 1], EPS, a, ALU.add, ALU.mult).then_inc(nw, 1)
                if step == 2:
                    v.tensor_scalar(c_, b_, -0.5, 1.5, ALU.mult, ALU.add).then_inc(nw, 1)
                if step == 3:
                    v.tensor_tensor(r, y, c_, ALU.mult).then_inc(nw, 1)

            def normalise(dst, src, n, k, wait):
                dve.wait_ge(S[("nw", "nw2")[k]], 4 * n + 4)
                if wait is not None:
                    dve.wait_ge(*wait)
                for tt in range(TT):
                    v.tensor_scalar(dst[:, tt], src[:, tt], mv[:, k, tt, 0:1], nt[:, k, 4, tt:tt + 1],
                                    ALU.subtract, ALU.mult).then_inc(S[("xn_s", "xn2_s")[k]], 1)

            def part_rest(n, i, first):
                order = ORDER.index(i)
                dve.wait_ge(S["p1"], 4 * n + order + 1)
                if not (first and order < 2):
                    dve.wait_ge(S["p3"], 4 * n + order - 1)
                v.scalar_tensor_tensor(rest[:, i % 2, :], M[:], bqk[:, i:i + 1], parts[:, i, 0, :],
                                       ALU.add, ALU.subtract).then_inc(S["r_s"], 1)

            def v_copy(n, h, first):
                dve.wait_ge(S["v_ps"], 2 * n + h + 1)
                if not first and h == 0:
                    dve.wait_ge(S["vaug_s"], 4 * n)
                v.tensor_tensor(vn[:, 2 * h:2 * h + 2], Mrow, bvb[:].rearrange("p (a d) -> p a d", a=1)
                                .to_broadcast([P, 2, D]), ALU.add).then_inc(S["v_sb"], 1)

            def reduce(b, h, j, nh):
                k = (16 * b + h) * 4 + j
                dve.wait_ge(S["a_done"], k + 1)
                v.tensor_reduce(mx[:, (h // 4) % 2, h % 4, j:j + 1], A[:, j, :], AX.X, ALU.max).then_inc(S["red"], 1)

            def negate(G):
                dve.wait_ge(S["maxT"], G + 1)
                v.tensor_scalar(mneg[:, 0, :], M[0:16, 0:P], -1.0, None, ALU.mult).then_inc(S["neg"], 1)
                dve.wait_ge(S["neg"], 2 * G + 1)
                v.scalar_tensor_tensor(mneg[:, 1, :], M[0:16, 0:P], -1.0, mneg[:, 0, :], ALU.mult,
                                       ALU.subtract).then_inc(S["neg"], 1)

            def attend(G, g, b, first):
                dve.wait_ge(S["pvt"], G + 1)
                v.reciprocal(rec[:], A4[:, :, :, DH]).then_inc(S["rec_s"], 1)
                dve.wait_ge(S["rec_s"], G + 1)
                if not first and g == 0:
                    dve.wait_ge(S["attnT_ps"], 2 * b)
                v.tensor_tensor(attn[:, :, 64 * g:64 * g + 64].rearrange("p q (j d) -> p q j d", j=4),
                                A4[:, :, :, 0:DH], rec[:].rearrange("p q (j a) -> p q j a", a=1)
                                .to_broadcast([P, TT, 4, DH]), ALU.mult).then_inc(S["attn_g"], 1)

            def add_residual(t, h, first):
                dve.wait_ge(S["o_ps"], 2 * t + h + 1)
                dve.wait_ge(S["xb"], t + 1)
                if not first and h == 0:
                    dve.wait_ge(S["x1_st"], 16 * t)
                v.tensor_tensor(x1[:, 2 * h:2 * h + 2], Mrow, xr[:, 2 * h:2 * h + 2], ALU.add).then_inc(S["x1_s"], 1)

            def bc(a):
                return a.rearrange("p (t a) -> p t a", a=1).to_broadcast([P, TT, E])

            def route(t, step):
                if step:
                    dve.wait_ge(S["rtc"], RT * t + step)
                if step == 0:
                    dve.wait_ge(S["lg_ps"], t + 1)
                    i_ = v.tensor_copy(lg[:], M[:, 0:TT * E].rearrange("p (t e) -> p t e", e=E))
                if step == 1:
                    i_ = v.tensor_reduce(sm[:, 0], lg[:], AX.X, ALU.max)
                if step == 2:
                    i_ = v.tensor_tensor(rt[:, 0], lg[:], bc(sm[:, 0]), ALU.subtract)
                if step == 3:
                    i_ = v.tensor_scalar(rt[:, 2], rt[:, 0], 0.0, float(E), ALU.is_lt, ALU.mult)
                if step == 4:
                    i_ = v.tensor_tensor(rt[:, 3], rt[:, 2], iota_e[:], ALU.add)
                if step == 5:
                    i_ = v.tensor_reduce(sm[:, 1], rt[:, 3], AX.X, ALU.min)
                if step == 6:
                    i_ = v.tensor_tensor(rt[:, 4], iota_e[:], bc(sm[:, 1]), ALU.is_equal)
                if step == 7:
                    i_ = v.scalar_tensor_tensor(rt[:, 5], rt[:, 4], -1e30, lg[:], ALU.mult, ALU.add)
                if step == 8:
                    i_ = v.tensor_reduce(sm[:, 2], rt[:, 5], AX.X, ALU.max)
                if step == 9:
                    i_ = v.tensor_tensor(rt[:, 6], rt[:, 5], bc(sm[:, 2]), ALU.subtract)
                if step == 10:
                    i_ = v.tensor_scalar(rt[:, 7], rt[:, 6], 0.0, float(E), ALU.is_lt, ALU.mult)
                if step == 11:
                    i_ = v.tensor_tensor(rt[:, 8], rt[:, 7], iota_e[:], ALU.add)
                if step == 12:
                    i_ = v.tensor_reduce(sm[:, 3], rt[:, 8], AX.X, ALU.min)
                if step == 13:
                    i_ = v.tensor_tensor(rt[:, 9], iota_e[:], bc(sm[:, 3]), ALU.is_equal)
                if step == 14:
                    i_ = v.tensor_tensor(mask[:], rt[:, 4], rt[:, 9], ALU.add)
                i_.then_inc(S["rtc"], 1)

            def weights(t):
                k = 0

                def link(i_):
                    nonlocal k
                    k += 1
                    i_.then_inc(S["tail_a"], 1)
                    dve.wait_ge(S["tail_a"], 10 * t + k)

                dve.wait_ge(S["ex"], t + 1)
                link(v.tensor_reduce(sm[:, 4], rt[:, 1], AX.X, ALU.add))
                link(v.reciprocal(sm[:, 5], sm[:, 4]))
                link(v.tensor_tensor(rt[:, 10], rt[:, 1], rt[:, 9], ALU.mult))
                link(v.tensor_reduce(sm[:, 6], rt[:, 10], AX.X, ALU.add))
                link(v.tensor_tensor(sm[:, 7], sm[:, 6], sm[:, 5], ALU.mult))
                link(v.scalar_tensor_tensor(sm[:, 8], sm[:, 5], 1e-9, sm[:, 7], ALU.add, ALU.add))
                link(v.reciprocal(sm[:, 9], sm[:, 8]))
                link(v.tensor_tensor(sm[:, 10], sm[:, 5], sm[:, 9], ALU.mult))
                link(v.tensor_tensor(sm[:, 11], sm[:, 7], sm[:, 9], ALU.mult))
                v.tensor_tensor(rt[:, 11], rt[:, 4], bc(sm[:, 10]), ALU.mult)
                link(v.tensor_tensor(rt[:, 12], rt[:, 9], bc(sm[:, 11]), ALU.mult))
                v.tensor_tensor(row[:, :, W_CW:W_CW + E], rt[:, 11], rt[:, 12], ALU.add).then_inc(S["cw_s"], 1)

            def places(t, first):
                k = 0

                def link(i_):
                    nonlocal k
                    k += 1
                    i_.then_inc(S["tail_b"], 1)
                    dve.wait_ge(S["tail_b"], 6 * t + k)

                dve.wait_ge(S["rank_ps"], t + 1)
                C = M[:, 0:TT * E].rearrange("p (t e) -> p t e", e=E)
                link(v.tensor_tensor(rt[:, 10], C, base[:, 0:1].to_broadcast([P, TT, E]), ALU.add))
                link(v.tensor_tensor(base[:, 0], M[:, TT * E:TT * E + E], base[:, 0], ALU.add))
                link(v.tensor_tensor(rt[:, 11], rt[:, 10], region[:], ALU.add))
                v.tensor_tensor(rt[:, 12], rt[:, 11], rt[:, 4], ALU.mult)
                link(v.tensor_tensor(rt[:, 13], rt[:, 11], rt[:, 9], ALU.mult))
                link(v.tensor_reduce(slots[:], rt[:, 12:14].rearrange("p a t e -> p (a t) e"), AX.X, ALU.add))
                if not first:
                    dve.wait_ge(S["sct"], 128 * t)
                v.tensor_copy(slots_u[:], slots[:]).then_inc(S["slot"], 1)
                link(v.tensor_copy(base[:, 1], base[:, 0]))

            def batch(b, first, last):
                n, t = b + 1, b - 1
                second = isinstance(b, int) and b == 1
                for s in range(STEPS):
                    if s == 2 and not first:
                        attend(4 * b - 1, 3, t, False)
                    if s in (4, 5) and not last:
                        part_rest(n, (None, None, None, None, 2, 0)[s], False)
                    if s == 7 and not last:
                        v_copy(n, 0, False)
                    if s == 8 and not first:
                        add_residual(t, 0, second)
                    if s == 10:
                        attend(4 * b + 1, 1, b, first)
                    if s == 14 and not first:
                        route(t, 0)
                    for j in range(4):
                        if not last or s + LEAD < STEPS:
                            reduce(b, s + LEAD, j, 0)
                        if s == 0 and not last:
                            stats_of(xt, n, 0, j, (S["x_in"], 16 * (n + 1)) if j == 0 else None)
                        if s == 1 and j == 0 and not last:
                            aggregate(n, 0)
                        if (s, j) in ((2, 0), (2, 1), (2, 2), (2, 3)) and not last:
                            newton(n, 0, j)
                        if s == 9 and not first:
                            stats_of(x1, t, 1, j, (S["x1_s"], 2 * t + 2) if j == 0 else None)
                        if s == 10 and j == 0 and not first:
                            aggregate(t, 1)
                        if s == 11 and not first:
                            newton(t, 1, j)
                        if s == 14 and not first:
                            for k in range(3):
                                route(t, 1 + 3 * j + k)
                        if s == 15 and j < 2 and not first:
                            route(t, 13 + j)
                    if s == 2 and not last:
                        normalise(xn, xt, n, 0, (S["xnT_ps"], 2 * n))
                    if s % 4 == 1 and not (last and s == 13):
                        negate(4 * b + s // 4 + 1)
                    if s in (4, 5) and not last:
                        part_rest(n, (None, None, None, None, 3, 1)[s], False)
                    if s == 6:
                        attend(4 * b, 0, b, first)
                    if s == 7 and not last:
                        v_copy(n, 1, False)
                    if s == 8 and not first:
                        add_residual(t, 1, second)
                    if s == 11 and not first:
                        normalise(xn2, x1, t, 1, None if second else (S["xl"], t))
                    if s == 15:
                        if not first:
                            places(t, second)
                        attend(4 * b + 2, 2, b, first)
                        if not first:
                            weights(t)

            for tt in range(TT):
                stats_of(xt, 0, 0, tt, (S["x_in"], 16))
            aggregate(0, 0)
            for k in range(4):
                newton(0, 0, k)
            normalise(xn, xt, 0, 0, None)
            dve.wait_ge(S["cin"], 16 * 11)
            dve.wait_ge(S["consts"], 1)
            for i in ORDER:
                part_rest(0, i, True)
            for h in range(2):
                v_copy(0, h, True)
            for h in range(LEAD):
                for j in range(4):
                    reduce(0, h, j, 0)
                if h == 3:
                    negate(0)

            batch(0, True, False)
            batch(1, False, False)
            with dve.Fori(2, B - 1) as b:
                batch(b, False, False)
            batch(B - 1, False, True)
            t = B - 1
            attend(4 * B - 1, 3, t, False)
            add_residual(t, 0, False)
            add_residual(t, 1, False)
            for j in range(TT):
                stats_of(x1, t, 1, j, (S["x1_s"], 2 * t + 2))
            aggregate(t, 1)
            for k in range(4):
                newton(t, 1, k)
            normalise(xn2, x1, t, 1, (S["xl"], t))
            for k in range(RT):
                route(t, k)
            places(t, False)

            kf = 0

            def link(i_):
                nonlocal kf
                kf += 1
                i_.then_inc(S["fin"], 1)
                dve.wait_ge(S["fin"], kf)

            link(v.tensor_copy(cnt_i[:, 0], base[:, 1]))
            link(v.tensor_scalar(cnt_f[:, 0], base[:, 1], float(P - 1), float(P), ALU.add, ALU.max))
            link(v.tensor_copy(cnt_i[:, 1], cnt_f[:, 0]))
            link(v.tensor_scalar(cnt_i[:, 2], cnt_i[:, 1], 7, None, ALU.logical_shift_right))
            link(v.tensor_copy(cnt_f[:, 1], cnt_i[:, 2]))
            link(v.memset(cnt_f[:, 0], 1.0))
            link(v.tensor_tensor_scan(cnt_f[:, 2], cnt_f[:, 0], cnt_f[:, 1], 0.0, ALU.mult, ALU.add))
            link(v.memset(tab[:, 0, 0:1], 0))
            link(v.tensor_copy(tab[:, 0, 1:E + 1], cnt_f[:, 2]))
            link(v.tensor_copy(tab[:, 1, 0:E], cnt_i[:, 0]))
            v.memset(ys[:], 0.0).then_inc(S["tabs"], 1)
            weights(t)

            dve.wait_ge(S["qk_ps"], 4 * B)
            v.memset(xT[:], 0.0).then_inc(S["xT_s"], 1)
            v.memset(hh, 0.0).then_inc(S["hh_s"], 2)
            v.memset(hl, 0.0).then_inc(S["hl_s"], 2)
            v.memset(meta_cw[:], 0.0).then_inc(S["y_s"], 1)
            dve.wait_ge(S["xT_s"], 1)
            dve.wait_ge(S["hh_s"], 2)
            dve.wait_ge(S["hl_s"], 2)
            dve.wait_ge(S["tabs"], 1)
            last = dve.value_load(tab[0:1, 0, E:E + 1], min_val=8, max_val=72)

            def xT_copy(i):
                dve.wait_ge(S["t_ps"], i + 1)
                v.tensor_copy(xT[:], XT16).then_inc(S["xT_s"], 1)

            def h_split(i, wait_s2):
                for k in range(2):
                    c = slice(T * k, T * k + T)
                    dve.wait_ge(S["gelu"], 2 * i + k + 3)
                    if wait_s2:
                        dve.wait_ge(S["s2"], i)
                    v.tensor_copy(hh[:, c], hf[:, c]).then_inc(S["hh_s"], 1)
                    dve.wait_ge(S["hh_s"], 2 * i + k + 3)
                    v.tensor_tensor(hl[:, c], hf[:, c], hh[:, c], ALU.subtract).then_inc(S["hl_s"], 1)

            def y_scale(i):
                dve.wait_ge(S["s2"], i + 1)
                dve.wait_ge(S["meta"], 32 * i + 32)
                dve.wait_ge(S["scat"], 16 * i + 16)
                v.tensor_scalar(ys[:], PV[:, 0:D], meta_cw[:, 0:1], 1.0 / WSC, ALU.mult,
                                ALU.mult).then_inc(S["y_s"], 1)

            xT_copy(0)
            xT_copy(1)
            h_split(0, False)
            with dve.Fori(1, last) as i:
                xT_copy(i + 1)
                y_scale(i - 1)
                h_split(i, True)
            y_scale(last - 1)

        @block.tensor
        def _(pe):
            mm, tr = nc.tensor.matmul, nc.tensor.transpose
            pe.wait_ge(S["cin"], 16 * 11)
            pe.wait_ge(S["consts"], 1)

            def xnT_piece(n, c, after):
                pe.wait_ge(*after)
                pe.wait_ge(S["xn_s"], TT * (n + 1))
                for tt in range(TT):
                    i_ = tr(M[:, P * tt:P * tt + P], xn[:, tt, P * c:P * c + P], ident[:])
                i_.then_inc(S["xnT_ps"], 1)

            def qk_piece(n, i, after):
                pe.wait_ge(*after)
                pe.wait_ge(S["xnT_sb"], 2 * n + 2)
                if i >= 2:
                    pe.wait_ge(S["ct_in"], 16 * (n + 1))
                w, src = ((wq, xnT), (wk, ct))[i // 2]
                h = i % 2
                for c in range(KC):
                    i_ = mm(M[:], w[:, c, P * h:P * h + P], src[:, c, :], start=(c == 0), stop=(c == KC - 1))
                i_.then_inc(S["qk_ps"], 1)

            def v_piece(n, h, after):
                pe.wait_ge(*after)
                for q in range(2):
                    t_ = 2 * h + q
                    for c in range(KC):
                        i_ = mm(Mrow[:, q], ct[:, c, P * t_:P * t_ + P], wv[:, c, :], start=(c == 0), stop=(c == KC - 1))
                i_.then_inc(S["v_ps"], 1)

            def max_piece(G, par, after):
                pe.wait_ge(*after)
                pe.wait_ge(S["red"], 16 * G + 16)
                tr(M[0:16, 0:P], mx[:, par].rearrange("p h t -> p (h t)"), ident[:]).then_inc(S["maxT"], 1)

            def pvt_piece(G, after):
                pe.wait_ge(*after)
                pe.wait_ge(S["pve"], G + 1)
                for q in range(TT):
                    i_ = tr(M[:, P * q:P * q + P], pvs[:, P * q:P * q + P], ident[:])
                i_.then_inc(S["pvt"], 1)

            def attnT_piece(t, c, after):
                pe.wait_ge(*after)
                pe.wait_ge(S["attn_g"], 4 * (t + 1))
                for tt in range(TT):
                    i_ = tr(M[:, P * tt:P * tt + P], attn[:, tt, P * c:P * c + P], ident[:])
                i_.then_inc(S["attnT_ps"], 1)

            def o_piece(t, h, after):
                pe.wait_ge(*after)
                pe.wait_ge(S["attnT_sb"], 2 * t + 2)
                for q in range(2):
                    t_ = 2 * h + q
                    for c in range(KC):
                        i_ = mm(Mrow[:, q], attnT[:, c, P * t_:P * t_ + P], wo[:, c, :], start=(c == 0), stop=(c == KC - 1))
                i_.then_inc(S["o_ps"], 1)

            def xn2T_piece(t, c, after):
                pe.wait_ge(*after)
                pe.wait_ge(S["xn2_s"], TT * (t + 1))
                for tt in range(TT):
                    i_ = tr(M[:, P * tt:P * tt + P], xn2[:, tt, P * c:P * c + P], ident[:])
                i_.then_inc(S["xn2T_ps"], 1)

            def lgT_piece(t, after):
                pe.wait_ge(*after)
                pe.wait_ge(S["xn2T_sb"], 2 * t + 2)
                for c in range(KC):
                    i_ = mm(M[0:E, :], rw[:, c, :], xn2T[:, c, :], start=(c == 0), stop=(c == KC - 1))
                i_.then_inc(S["lgT_ps"], 1)

            def lg_piece(t):
                wait(pe, S["lgT_sb"], t + 1)
                for tt in range(TT):
                    i_ = tr(M[:, E * tt:E * tt + E], lgT[:, P * tt:P * tt + P], ident[0:E, 0:E])
                i_.then_inc(S["lg_ps"], 1)

            def rank_piece(t):
                pe.wait_ge(S["rtc"], RT * (t + 1))
                mk = mask[:].rearrange("p t e -> p (t e)")
                mm(M[:, 0:TT * E], tri[:], mk, start=True, stop=False, skip_group_check=True)
                for k in range(1, TT):
                    mm(M[:, k * E:TT * E], ones[:], mk[:, 0:(TT - k) * E], start=False, stop=False, skip_group_check=True)
                for k in range(TT):
                    i_ = mm(M[:, TT * E:TT * E + E], ones[:], mk[:, k * E:k * E + E], start=False,
                            stop=(k == TT - 1), skip_group_check=True)
                i_.then_inc(S["rank_ps"], 1)

            def score_a(b, h, j):
                g = (h // 4) % 4
                if j == 0 and h % 4 == 0:
                    pe.wait_ge(qk_in[g], 96 * (b + 1 + h // 16))
                if not (isinstance(b, int) and b == 0 and h == 0):
                    pe.wait_ge(S["red"], (16 * b + h) * 4 + j - 3)
                mm(A[:, j, :], qst[0:KS, g, h % 4, P * j:P * j + P], kst[0:KS, g, h % 4, :],
                   start=True, stop=True).then_inc(S["a_done"], 1)

            def score_b(b, s, j, first):
                g, kc = s // 4, s % 4
                if kc == 0 and j == 0:
                    pe.wait_ge(mrow[g], 32 * (b + 1))
                if not (first and s == 0 and j < 2):
                    pe.wait_ge(S["exp"], (16 * b + s) * 4 + j - 1)
                mm(Bp[:, j % 2, :], kst[0:KM, g, j, P * kc:P * kc + P], qst[0:KM, g, j, :],
                   start=True, stop=True).then_inc(S["b_done"], 1)

            def values(b, s, first):
                g, kc = (s // 4) % 4, s % 4
                pe.wait_ge(S["exp"], (16 * b + s) * 4 + 4)
                if kc == 0:
                    pe.wait_ge(S["vaug_s"], 4 * b + g + 1)
                    if not (first and s == 0):
                        pe.wait_ge(S["pve"], 4 * b + g)
                for j in range(4):
                    i_ = mm(PV[32 * j:32 * j + 32, :], vaug[:, g, kc, j, :], pT[:, s % 2, j, :],
                            start=(kc == 0), stop=(kc == 3))
                i_.then_inc(S["pv"], 1)

            def batch(b, first, last):
                n, t = b + 1, b - 1
                for s in range(STEPS):
                    if s == 2 and not first:
                        pvt_piece(4 * b - 1, (S["neg"], 2 * (4 * b + 1) + 2))
                    if s == 3 and not last:
                        xnT_piece(n, 0, (S["neg"], 2 * (4 * b + 1) + 2) if first else (S["attn_g"], 4 * b))
                    if s == 4 and not last:
                        qk_piece(n, 2, (S["xnT_sb"], 2 * n + 2))
                    if s == 5 and not last:
                        qk_piece(n, 0, (S["r_s"], 4 * n + 2))
                    if s == 6 and not first:
                        attnT_piece(t, 0, (S["neg"], 2 * (4 * b + 2) + 2) if last else (S["r_s"], 4 * n + 4))
                    if s == 7 and not last:
                        v_piece(n, 0, (S["attn_g"], 4 * b + 1))
                    if s == 8 and not first:
                        o_piece(t, 0, (S["attn_g"], 4 * b + 1) if last else (S["v_sb"], 2 * n + 2))
                    if s == 10:
                        pvt_piece(4 * b + 1, (S["neg"], 2 * (4 * b + 3) + 2))
                    if s == 12 and not first:
                        xn2T_piece(t, 0, (S["attn_g"], 4 * b + 2))
                    if s == 13 and not first:
                        lgT_piece(t, (S["xn2T_sb"], 2 * t + 2))
                    if s == 14 and not first:
                        if not last:
                            wait(pe, S["neg"], 2 * (4 * b + 4) + 2)
                        lg_piece(t)
                    for j in range(4):
                        if not last or s + LEAD < STEPS:
                            score_a(b, s + LEAD, j)
                        score_b(b, s, j, first)
                    if s % 4 == 1 and not (last and s == 13):
                        G = 4 * b + s // 4 + 1
                        if s == 1:
                            after = (S["neg"], 2) if first else (S["attn_g"], 4 * b - 1)
                        if s == 5:
                            after = (S["neg"], 2 * G) if last else (S["r_s"], 4 * n + 3)
                            if last:
                                after = (S["attn_g"], 4 * b)
                        if s == 9:
                            after = (S["v_sb"], 2 * n + 2) if first else (S["x1_s"], 2 * t + 2)
                        if s == 13:
                            after = (S["attn_g"], 4 * b + 2) if first else (S["lgT_sb"], t + 1)
                        max_piece(G, (s // 4 + 1) % 2, after)
                    if s == 3 and not last:
                        xnT_piece(n, 1, (S["xnT_sb"], 2 * n + 1))
                    if s == 4 and not last:
                        qk_piece(n, 3, (S["r_s"], 4 * n + 1))
                    if s == 5 and not last:
                        qk_piece(n, 1, (S["neg"], 2 * (4 * b + 2) + 2))
                    if s == 6:
                        if not first:
                            attnT_piece(t, 1, (S["attnT_sb"], 2 * t + 1))
                        pvt_piece(4 * b, (S["r_s"], 4 * n + 4) if first else (S["attnT_sb"], 2 * t + 2))
                    if s == 7 and not last:
                        v_piece(n, 1, (S["v_sb"], 2 * n + 1))
                    if s == 8 and not first:
                        o_piece(t, 1, (S["x1_s"], 2 * t + 1))
                    if s == 12 and not first:
                        xn2T_piece(t, 1, (S["xn2T_sb"], 2 * t + 1))
                    if s == 15:
                        if not first:
                            rank_piece(t)
                            pvt_piece(4 * b + 2, (S["slot"], t + 1))
                        else:
                            pvt_piece(4 * b + 2, (S["neg"], 2 * (4 * b + 4) + 2))
                    if not (first and s == 0):
                        values(b, s - 1, first)

            for c in range(KC):
                xnT_piece(0, c, (S["xn_s"], TT) if c == 0 else (S["xnT_sb"], 1))
            for k, i in enumerate((2, 3, 0, 1)):
                qk_piece(0, i, (S["xnT_sb"], 2) if k == 0 else (S["r_s"], k))
            for h in range(2):
                v_piece(0, h, (S["r_s"], 4) if h == 0 else (S["v_sb"], 1))
            for h in range(LEAD):
                for j in range(4):
                    if h == 0:
                        if j == 0:
                            pe.wait_ge(qk_in[0], 96)
                        mm(A[:, j, :], qst[0:KS, 0, 0, P * j:P * j + P], kst[0:KS, 0, 0, :],
                           start=True, stop=True).then_inc(S["a_done"], 1)
                    else:
                        score_a(0, h, j)
                if h == 3:
                    max_piece(0, 0, (S["v_sb"], 2))

            batch(0, True, False)
            batch(1, False, False)
            with pe.Fori(2, B - 1) as b:
                batch(b, False, False)
            batch(B - 1, False, True)
            t = B - 1
            values(B, -1, False)
            pvt_piece(4 * B - 1, (S["attn_g"], 4 * B - 1))
            attnT_piece(t, 0, (S["attn_g"], 4 * B))
            attnT_piece(t, 1, (S["attnT_sb"], 2 * t + 1))
            o_piece(t, 0, (S["attnT_sb"], 2 * t + 2))
            o_piece(t, 1, (S["x1_s"], 2 * t + 1))
            xn2T_piece(t, 0, (S["x1_s"], 2 * t + 2))
            xn2T_piece(t, 1, (S["xn2T_sb"], 2 * t + 1))
            lgT_piece(t, (S["xn2T_sb"], 2 * t + 2))
            lg_piece(t)
            rank_piece(t)

            def turn(i):
                pe.wait_ge(S["xrow_in"], 16 * i + 16)
                pe.wait_ge(S["xT_s"], i + 1)
                for c in range(4):
                    i_ = tr(XT16[:, P * c:P * c + P], xrow16[:, P * c:P * c + P], ident16[:])
                i_.then_inc(S["t_ps"], 1)

            def up(i, q):
                pe.wait_ge(S["xT_s"], i + 2)
                for k in range(2):
                    pe.wait_ge(S["gelu"], 2 * i + k + 1)
                    for m in range(4):
                        hc = 4 * k + m
                        terms = [(wp, c, xp) for c in range(KC) for wp, xp in ((0, 0), (0, 1), (1, 0))]
                        for z, (wp, c, xp) in enumerate(terms):
                            i_ = mm(A[:, k, P * m:P * m + P],
                                    whl[q][:, (2 * wp + c) * HID + P * hc:(2 * wp + c) * HID + P * hc + P],
                                    xT[:, (2 * xp + c) * P:(2 * xp + c) * P + P], start=(z == 0), stop=(z == 5))
                    i_.then_inc(S["s1"], 1)

            def down(i, q):
                pe.wait_ge(S["y_s"], i + 1)
                for k in range(2):
                    pe.wait_ge(S["hl_s"], 2 * i + k + 3)
                    for m in range(4):
                        hc = 4 * k + m
                        for z, (hp, wp) in enumerate(((hh, 0), (hh, 1), (hl, 0))):
                            at = (4 + 2 * wp) * HID + D * hc
                            i_ = mm(PV[:, 0:D], hp[:, P * hc:P * hc + P], whl[q][:, at:at + D],
                                    start=(hc == 0 and z == 0), stop=(hc == HC - 1 and z == 2))
                i_.then_inc(S["s2"], 1)

            pe.wait_ge(S["tabs"], 1)
            pe.wait_ge(S["pve"], 4 * B)
            pe.wait_ge(S["slot"], B)
            pe.wait_ge(S["red"], 64 * B)

            def expert(pair, q, first):
                e = 2 * pair + q
                lo = pe.value_load(tab[0:1, 0, bass.ds(e, 1)], min_val=0, max_val=71)
                hi = pe.value_load(tab[0:1, 0, bass.ds(e + 1, 1)], min_val=1, max_val=72)
                pe.wait_ge(wld[q], 16 * (pair + 1))
                up(lo, q)
                turn(lo + 1)
                if not first:
                    down(lo - 1, 1 - q)
                with pe.If(lo + 1 < hi):
                    with pe.Fori(lo + 1, hi) as i:
                        up(i, q)
                        turn(i + 1)
                        down(i - 1, q)
                with pe.Else():
                    pass

            turn(0)
            expert(0, 0, True)
            expert(0, 1, False)
            with pe.Fori(1, E // 2) as pair:
                expert(pair, 0, False)
                expert(pair, 1, False)
            last = pe.value_load(tab[0:1, 0, E:E + 1], min_val=8, max_val=72)
            down(last - 1, 1)


RT = 15

_INS = ["x", "ctxT", "wqT", "wkT", "wvT", "woT", "bq", "bk", "bv", "bo", "rwT", "w1", "w2"]


def kernel(x, ctx_1024, L0_xattn_wq_w, L0_xattn_wq_b, L0_xattn_wk_w, L0_xattn_wk_b, L0_xattn_wv_w, L0_xattn_wv_b,
           L0_xattn_wo_w, L0_xattn_wo_b, L0_ffn_router_w, L0_ffn_w1, L0_ffn_w2):
    import numpy as np
    import concourse.bacc as bacc
    from concourse.bass_utils import run_bass_kernel_spmd

    arrays = {
        "x": x, "ctxT": np.transpose(np.asarray(ctx_1024), (0, 2, 1)),
        "wqT": np.asarray(L0_xattn_wq_w).T, "wkT": np.asarray(L0_xattn_wk_w).T,
        "wvT": np.asarray(L0_xattn_wv_w).T, "woT": np.asarray(L0_xattn_wo_w).T,
        "bq": L0_xattn_wq_b, "bk": L0_xattn_wk_b, "bv": L0_xattn_wv_b, "bo": L0_xattn_wo_b,
        "rwT": np.asarray(L0_ffn_router_w).T, "w1": L0_ffn_w1, "w2": L0_ffn_w2,
    }
    nc = bacc.Bacc("TRN2", target_bir_lowering=False, num_devices=1)
    ins, args = {}, []
    for name in _INS:
        a = np.ascontiguousarray(arrays[name])
        ins[f"in_{name}"] = a
        args.append(nc.dram_tensor(f"in_{name}", a.shape, mybir.dt.from_np(a.dtype), kind="ExternalInput").ap())
    out = nc.dram_tensor("out_rows", (N + P, D), F32, kind="ExternalOutput").ap()
    build(nc, *args, out)
    r = run_bass_kernel_spmd(nc, [ins], core_ids=[0])
    return r.results[0]["out_rows"][0:N].reshape(B, T, D)
```

```python
from contextlib import ExitStack

import concourse.bass as bass
from concourse import mybir

F32 = mybir.dt.float32
F16 = mybir.dt.float16
BF16 = mybir.dt.bfloat16
I32 = mybir.dt.int32
U32 = mybir.dt.uint32
ALU = mybir.AluOpType
ACT = mybir.ActivationFunctionType
AX = mybir.AxisListType

P = 128
B, T, D = 8, 512, 256
NH, DH = 16, 16
KC = D // P
TT = T // P
E, HID = 8, 1024
HC = HID // P
N = B * T
REGION = N + P
XW = D
W_CW, W_ID, ROWW = XW, XW + E, XW + E + 1
WSC = 256.0
PARTS = 3
RUNS = ((0, 48, 0, 3), (48, 32, 0, 2), (80, 16, 0, 1))
KRUNS = ((0, 48, 0, 3), (48, 32, 1, 3), (80, 16, 2, 3))
ORDER = (2, 3, 0, 1)
KS, KM = 96, 98
QK_STEPS = (1, 3, 4, 5)
STEPS = 16
LEAD = 7
EPS = 1e-5
MAXT = 2 * N // P + E
TN = MAXT + 2


def build(nc, x, ctxT, wqT, wkT, wvT, woT, bq, bk, bv, bo, rwT, w1, w2, out):
    scr = [nc.dram_tensor(f"scr_{n}", [B, NH, PARTS, DH, T], BF16).ap() for n in "qk"]
    wsp = nc.dram_tensor("wsp", [E, P, 8 * HID], F16).ap()
    rows_d = nc.dram_tensor("rows_d", [E * REGION, ROWW], F32).ap()

    with ExitStack() as ctx:
        def sb(name, shape, dt=F32):
            return ctx.enter_context(nc.sbuf_tensor(name, shape, dt))

        def ps(name, shape, dt=F32):
            return ctx.enter_context(nc.psum_tensor(name, shape, dt))

        def sem(name):
            return ctx.enter_context(nc.semaphore(name))

        ident = sb("ident", [P, P])
        ident16 = sb("ident16", [P, P], F16)
        tri = sb("tri", [P, P], BF16)
        ones = sb("ones", [P, P], BF16)
        iota_e = sb("iota_e", [P, TT, E])
        region = sb("region", [P, TT, E])
        tok_id = sb("tok_id", [P, B * TT], I32)
        pad_row = sb("pad_row", [P, ROWW])
        wq = sb("wq", [P, KC, D])
        wk = sb("wk", [P, KC, D])
        wv = sb("wv", [P, KC, D])
        wo = sb("wo", [P, KC, D])
        rw = sb("rw", [P, KC, E])
        bqk = sb("bqk", [P, 4])
        bvb = sb("bvb", [P, D])
        bob = sb("bob", [P, D])
        xt = sb("xt", [P, TT, D])
        xr = sb("xr", [P, TT, D])
        ct = sb("ct", [P, KC, T])
        xn = sb("xn", [P, TT, D])
        xnT = sb("xnT", [P, KC, T])
        parts = sb("parts", [P, 4, PARTS, T], BF16)
        rest = sb("rest", [P, 2, T])
        qst = sb("qst", [P, 4, 4, T], BF16)
        kst = sb("kst", [P, 4, 4, T], BF16)
        vn = sb("vn", [P, TT, D])
        vaug = sb("vaug", [P, 4, TT, 4, 32])
        pT = sb("pT", [P, 2, 4, T])
        pvs = sb("pvs", [P, T])
        attn = sb("attn", [P, TT, D])
        attnT = sb("attnT", [P, KC, T])
        x1 = sb("x1", [P, TT, D])
        xn2 = sb("xn2", [P, TT, D])
        xn2T = sb("xn2T", [P, KC, T])
        row = sb("row", [P, TT, ROWW])
        row16 = row[:, :, 0:XW].bitcast(F16)
        mx = sb("mx", [P, 2, 4, TT])
        mneg = sb("mneg", [16, 2, P], BF16)
        rec = sb("rec", [P, TT, 4])
        lgT = sb("lgT", [E, T])
        stats = sb("stats", [P, 2, TT, 6])
        mv = sb("mv", [P, 2, TT, 2])
        lnv = sb("lnv", [P, 2, TT])
        nt = sb("nt", [P, 2, 5, TT])
        eps_t = sb("eps_t", [P, 1])
        warm = sb("warm", [P, 1])
        lg = sb("lg", [P, TT, E])
        rt = sb("rt", [P, 14, TT, E])
        sm = sb("sm", [P, 12, TT])
        mask = sb("mask", [P, TT, E], BF16)
        base = sb("base", [P, 2, E])
        slots = sb("slots", [P, 2 * TT])
        slots_u = sb("slots_u", [P, 2 * TT], U32)
        cnt_i = sb("cnt_i", [P, 4, E], I32)
        cnt_f = sb("cnt_f", [P, 3, E])
        tab = sb("tab_tiles", [P, 2, E + 1], I32)
        wst = sb("wst", [P, 4 * HID])
        wsh = sb("wsh", [P, 8 * HID], F16)
        whl = [sb(f"whl{q}", [P, 8 * HID], F16) for q in range(2)]
        hf = xt[:].rearrange("p a b -> p (a b)")
        hh = xnT[:].rearrange("p a b -> p (a b)").bitcast(F16)[:, 0:HID]
        hl = xnT[:].rearrange("p a b -> p (a b)").bitcast(F16)[:, HID:2 * HID]
        xrow = sb("xrow", [P, XW])
        xrow16 = xrow[:].bitcast(F16)
        xT = sb("xT", [P, 4 * P], F16)
        meta_cw = sb("meta_cw", [P, 1])
        meta_in = sb("meta_in", [P, 1], U32)
        meta_id = sb("meta_id", [P, 1], U32)
        iota_t = sb("iota_t", [P, TN])
        tt_f = wst[:, 0:2 * TN * (E - 1)].rearrange("p (a t e) -> p a t e", a=2, e=E - 1)
        tt_s = wst[:, 2 * HID:2 * HID + 7 * TN].rearrange("p (a t) -> p a t", a=7)
        tile_tab = sb("tile_tab", [P, 2, TN], I32)
        ys = pvs[:, 0:D]

        A = ps("A", [P, 2, T])
        Bp = ps("Bp", [P, 2, T])
        PV = ps("PV", [P, T])
        M = [ps(f"M{m}", [P, T]) for m in range(3)]

        names = """consts cin cin_k c_exp x_in xr_in ct_in bn ag lnv_s y0 nw xn_s xnT_ps xnT_sb qk_ps p1 r_s p2 p3
            v_ps v_sb vaug_s a_done red b_done exp pv pve pvt rec_s attn_g attnT_ps attnT_sb o_ps x1_s xb x1_st
            bn2 ag2 lnv2 y02 nw2 xn2_s xh xl xn2T_ps xn2T_sb lgT_ps lgT_sb lg_ps rtc ex mask_s cw_s rank_ps slot
            idw sct maxT neg fin fin2 tabs padd w_in w_s w_h w_l wst_s wprep xrow_in t_ps xT_s s1 gelu hh_s hl_s s2 y_s
            meta scat outinit ponce wgt tail_b passed""".split()
        S = {k: sem("s_" + k) for k in names}
        st_part = [sem(f"s_st{i}") for i in range(4)]
        qk_in = [sem(f"s_qk{g}") for g in range(4)]
        mrow = [sem(f"s_mrow{g}") for g in range(4)]
        wld = [sem(f"s_wld{q}") for q in range(2)]

        def wait(eng, s, value):
            eng.wait_ge(s, value)
            if not isinstance(value, int):
                eng.sem_inc(S["passed"], 1)

        A4 = M[1][:].rearrange("p (q j r) -> p q j r", q=TT, j=4)
        XT16 = M[1][:].bitcast(F16)[:, 0:4 * P]

        def rows_of(m):
            return M[m][:].rearrange("p (a n) -> p a n", a=2)

        block = ctx.enter_context(nc.Block())

        @block.sync
        def _(sp):
            def load_w(w, src, sem_):
                sp.dma_start(w[:], src.rearrange("(c p) n -> p c n", p=P)).then_inc(sem_, 16)

            def load_x(b):
                sp.dma_start(xt[:], x[bass.ds(b, 1)].rearrange("a (t p) d -> p (a t) d", p=P)).then_inc(S["x_in"], 16)

            def load_ct(b):
                sp.dma_start(ct[:], ctxT[bass.ds(b, 1)].rearrange("a (c p) t -> p (a c) t", p=P)).then_inc(S["ct_in"], 16)

            def store_parts(n, i):
                dst, h = scr[i // 2], i % 2
                for c in range(PARTS):
                    wait(sp, (S["p1"], S["p2"], S["p3"])[c], 4 * n + i + 1)
                    at = c if i < 2 else PARTS - 1 - c
                    sp.dma_start(dst[bass.ds(n, 1), 8 * h:8 * h + 8, at].rearrange("a h d t -> (a h) d t"),
                                 parts[:, i, c, :]).then_inc(st_part[i], 16)

            def load_stack(n, g, first):
                for i in (g // 2, 2 + g // 2):
                    wait(sp, st_part[i], 48 * (n + 1))
                if not first:
                    wait(sp, S["b_done"], 64 * (n - 1) + 16 * (g + 1))
                for st, src, runs in ((qst, scr[0], RUNS), (kst, scr[1], KRUNS)):
                    for r0, nr, c0, c1 in runs:
                        sp.dma_start(st[r0:r0 + nr, g],
                                     src[bass.ds(n, 1), 4 * g:4 * g + 4, c0:c1].rearrange("a h c d t -> (c d) (a h) t")
                                     ).then_inc(qk_in[g], 16)

            def store_x1(t):
                wait(sp, S["x1_s"], 2 * t + 2)
                sp.dma_start(out[bass.ds(t * T, T)].rearrange("(t p) d -> p t d", p=P), x1[:]).then_inc(S["x1_st"], 16)

            def load_xr(t, first):
                if not first:
                    wait(sp, S["x1_s"], 2 * t)
                sp.dma_start(xr[:], x[bass.ds(t, 1)].rearrange("a (t p) d -> p (a t) d", p=P)).then_inc(S["xr_in"], 16)

            def prep(e, first):
                if not first:
                    wait(sp, S["w_l"], 2 * e)
                sp.dma_start(wst[:, 0:2 * HID].rearrange("p (c n) -> p c n", c=KC),
                             w1[bass.ds(e, 1)].rearrange("a (c p) n -> p (a c) n", p=P)).then_inc(S["w_in"], 16)
                sp.dma_start(wst[:, 2 * HID:4 * HID].rearrange("p (c n) -> p c n", c=HC),
                             w2[bass.ds(e, 1)].rearrange("a (c p) n -> p (a c) n", p=P)).then_inc(S["w_in"], 16)

            def prep_out(e):
                wait(sp, S["w_l"], 2 * e + 2)
                sp.dma_start(wsp[bass.ds(e, 1)].rearrange("a p n -> p (a n)"), wsh[:]).then_inc(S["wprep"], 16)

            load_w(wk, wkT, S["cin_k"])
            load_ct(0)
            load_x(0)
            for i, (bias, h) in enumerate(((bq, 0), (bq, 1), (bk, 0), (bk, 1))):
                sp.dma_start(bqk[:, i:i + 1], bias[h * P:h * P + P].rearrange("(p a) -> p a", a=1)).then_inc(S["cin_k"], 16)
            load_w(wq, wqT, S["cin"])
            load_w(wv, wvT, S["cin"])
            for t_, bias in ((bvb, bv), (bob, bo)):
                sp.dma_start(t_[:], bias.rearrange("(a n) -> a n", a=1).to_broadcast([P, D])).then_inc(S["cin"], 16)
            load_w(wo, woT, S["cin"])
            load_w(rw, rwT, S["cin"])
            wait(sp, S["xn_s"], TT)
            load_x(1)
            for i in ORDER:
                store_parts(0, i)
            wait(sp, S["v_ps"], 2)
            load_ct(1)
            for g in range(4):
                load_stack(0, g, True)

            def batch(b, first, last):
                n, t = b + 1, b - 1
                if not first:
                    load_stack(b, 3, False)
                    load_xr(t, first=(isinstance(b, int) and b == 1))
                prep(b, first)
                if not last:
                    for i in ORDER:
                        store_parts(n, i)
                    load_stack(n, 0, False)
                    wait(sp, S["xn_s"], TT * (n + 1))
                    load_x((b + 2) % B)
                    load_stack(n, 1, False)
                    wait(sp, S["v_ps"], 2 * (n + 1))
                    load_ct((b + 2) % B)
                if not first:
                    store_x1(t)
                if not last:
                    load_stack(n, 2, False)
                prep_out(b)

            batch(0, True, False)
            batch(1, False, False)
            with sp.Fori(2, B - 1) as b:
                batch(b, False, False)
            batch(B - 1, False, True)
            load_xr(B - 1, False)
            store_x1(B - 1)

            wait(sp, S["tabs"], 1)
            for e in range(E):
                c = sp.value_load(tab[0:1, 1, e:e + 1], min_val=0, max_val=N)
                sp.dma_start(rows_d[bass.ds(c + e * REGION, P)], pad_row[:]).then_inc(S["padd"], 16)
            wait(sp, S["padd"], 16 * E)
            wait(sp, S["tabs"], 2)
            wait(sp, S["sct"], 16 * 2 * TT * B)

            def row_at(i):
                return sp.value_load(tile_tab[0:1, 0, bass.ds(i, 1)], min_val=0, max_val=E * REGION - P)

            def load_row(i):
                at = row_at(i)
                wait(sp, S["xT_s"], i + 1)
                sp.dma_start(xrow[:], rows_d[bass.ds(at, P), 0:XW]).then_inc(S["xrow_in"], 16)

            def load_meta(i):
                at = row_at(i)
                e = sp.value_load(tile_tab[0:1, 1, bass.ds(i, 1)], min_val=0, max_val=E - 1)
                wait(sp, S["y_s"], 2 * i + 2)
                sp.dma_start(meta_cw[:], rows_d[bass.ds(at, P), bass.ds(e + W_CW, 1)],
                             allow_slow_non_contiguous=True).then_inc(S["meta"], 16)
                sp.dma_start(meta_in[:], rows_d[bass.ds(at, P), W_ID:W_ID + 1].bitcast(U32),
                             allow_slow_non_contiguous=True).then_inc(S["meta"], 16)

            load_row(0)
            load_row(1)
            last = sp.value_load(tab[0:1, 0, E:E + 1], min_val=8, max_val=MAXT)
            with sp.Fori(0, last) as i:
                load_row(i + 2)
                load_meta(i)
            wait(sp, S["xrow_in"], last * 16 + 32)
            wait(sp, S["scat"], last * 16 + 16)

        @block.gpsimd
        def _(pool):
            def once(instr, k):
                instr.then_inc(S["ponce"], 1)
                wait(pool, S["ponce"], k)

            once(nc.gpsimd.memset(ident[:], 0.0), 1)
            once(nc.gpsimd.affine_select(out=ident[:], in_=ident[:], compare_op=ALU.not_equal, fill=1.0, base=0,
                                         pattern=[[-1, P]], channel_multiplier=1), 2)
            once(nc.gpsimd.tensor_copy(ident16[:], ident[:]), 3)
            once(nc.gpsimd.memset(ones[:], 1.0), 4)
            once(nc.gpsimd.affine_select(out=tri[:], in_=ones[:], compare_op=ALU.is_ge, fill=0.0, base=-1,
                                         pattern=[[1, P]], channel_multiplier=-1), 5)
            once(nc.gpsimd.iota(iota_e[:], [[0, TT], [1, E]], base=0, channel_multiplier=0,
                                allow_small_or_imprecise_dtypes=True), 6)
            once(nc.gpsimd.iota(tok_id[:], [[P, B * TT]], base=0, channel_multiplier=1), 7)
            once(nc.gpsimd.memset(pad_row[:], 0.0), 8)
            once(nc.gpsimd.iota(pad_row[:, W_ID:W_ID + 1].bitcast(I32), [[1, 1]], base=N, channel_multiplier=1), 9)
            once(nc.gpsimd.memset(kst[KS:KM], 1.0), 10)
            once(nc.gpsimd.memset(vaug[:], 1.0), 11)
            once(nc.gpsimd.memset(base[:], 0.0), 12)
            once(nc.gpsimd.memset(eps_t[:], EPS), 13)
            once(nc.gpsimd.tensor_scalar(region[:], iota_e[:], float(REGION), None, ALU.mult), 14)
            once(nc.gpsimd.iota(iota_t[:], [[1, TN]], base=0, channel_multiplier=0,
                                allow_small_or_imprecise_dtypes=True), 15)
            wait(pool, S["cin"], 16 * 6)
            wait(pool, S["cin_k"], 16 * 5)
            once(nc.gpsimd.tensor_scalar(wq[:], wq[:], DH ** -0.5, None, ALU.mult), 16)
            nc.gpsimd.tensor_scalar(bqk[:, 0:2], bqk[:, 0:2], DH ** -0.5, None, ALU.mult).then_inc(S["consts"], 1)
            pool.dma_start(out[N:N + P], pad_row[:, 0:D]).then_inc(S["scat"], 16)

            def split(n, i, first):
                k = 4 * n + ORDER.index(i) + 1
                wait(pool, S["r_s"], k)
                if not first:
                    wait(pool, st_part[i], 48 * n)
                nc.gpsimd.tensor_copy(parts[:, i, 1, :], rest[:, i % 2, :]).then_inc(S["p2"], 1)
                wait(pool, S["p2"], k)
                nc.gpsimd.tensor_tensor(parts[:, i, 2, :], rest[:, i % 2, :], parts[:, i, 1, :],
                                        ALU.subtract).then_inc(S["p3"], 1)

            def values(n, g, first):
                wait(pool, S["v_sb"], 2 * n + 2)
                if not first:
                    wait(pool, S["pv"], 16 * (n - 1) + 4 * (g + 1))
                nc.gpsimd.tensor_copy(vaug[:, g, :, :, 0:DH],
                                      vn[:, :, 64 * g:64 * g + 64].rearrange("p t (h d) -> p t h d", h=4)
                                      ).then_inc(S["vaug_s"], 1)

            def expert_low(e, k):
                wait(pool, S["w_h"], 16 * e + 8 * k + 8)
                a, hi, lo = wst[:, 2 * HID * k:2 * HID * k + 2 * HID], 4 * HID * k, 4 * HID * k + 2 * HID
                nc.gpsimd.tensor_tensor(wsh[:, lo:lo + 2 * HID], a, wsh[:, hi:hi + 2 * HID],
                                        ALU.subtract).then_inc(S["w_l"], 1)

            def residual(t):
                wait(pool, S["xr_in"], 16 * (t + 1))
                nc.gpsimd.tensor_tensor(xr[:], xr[:], bob[:].rearrange("p (a d) -> p a d", a=1).to_broadcast([P, TT, D]),
                                        ALU.add).then_inc(S["xb"], 1)

            def rows(t, first):
                wait(pool, S["xn2_s"], TT * (t + 1))
                if not first:
                    wait(pool, S["sct"], 128 * t)
                nc.gpsimd.tensor_copy(row16[:, :, 0:D], xn2[:]).then_inc(S["xh"], 1)
                wait(pool, S["xh"], t + 1)
                nc.gpsimd.tensor_tensor(row16[:, :, D:2 * D], xn2[:], row16[:, :, 0:D], ALU.subtract).then_inc(S["xl"], 1)
                nc.gpsimd.tensor_copy(row[:, :, W_ID].bitcast(I32), tok_id[:, bass.ds(t * TT, TT)]).then_inc(S["idw"], 1)

            def scatter(t):
                wait(pool, S["slot"], t + 1)
                wait(pool, S["cw_s"], t + 1)
                wait(pool, S["xl"], t + 1)
                wait(pool, S["idw"], t + 1)
                for c in range(2):
                    for tt in range(TT):
                        pool.indirect_dma_start(
                            rows_d, bass.IndirectOffsetOnAxis(slots_u[:, c * TT + tt:c * TT + tt + 1], axis=0),
                            row[:, tt, :], None).then_inc(S["sct"], 16)

            for i in ORDER:
                split(0, i, True)
            for g in range(4):
                values(0, g, True)

            def batch(b, first, last):
                n, t = b + 1, b - 1
                if not first:
                    values(b, 3, False)
                    residual(t)
                if not last:
                    for i in ORDER:
                        split(n, i, False)
                if not first:
                    wait(pool, S["wprep"], 16 * b)
                expert_low(b, 0)
                if not first:
                    rows(t, first=(isinstance(b, int) and b == 1))
                expert_low(b, 1)
                if not last:
                    for g in range(3):
                        values(n, g, False)
                if not first:
                    scatter(t)

            batch(0, True, False)
            batch(1, False, False)
            with pool.Fori(2, B - 1) as b:
                batch(b, False, False)
            batch(B - 1, False, True)

            def load_weights(e, q):
                pool.dma_start(whl[q][:], wsp[bass.ds(e, 1)].rearrange("a p n -> p (a n)")).then_inc(wld[q], 16)

            load_weights(0, 0)
            load_weights(1, 1)
            residual(B - 1)
            rows(B - 1, False)
            scatter(B - 1)

            wait(pool, S["wprep"], 16 * E)
            wait(pool, S["tabs"], 1)
            wait(pool, S["x1_st"], 16 * B)

            def expert(e, q, first, last=False):
                lo = pool.value_load(tab[0:1, 0, bass.ds(e, 1)], min_val=0, max_val=MAXT - 1)
                hi = pool.value_load(tab[0:1, 0, bass.ds(e + 1, 1)], min_val=1, max_val=MAXT)
                if not first and not last:
                    wait(pool, S["s2"], lo)
                    load_weights(e + 1, 1 - q)
                with pool.Fori(lo, hi) as i:
                    wait(pool, S["y_s"], 2 * i + 4)
                    pool.indirect_dma_start(out, bass.IndirectOffsetOnAxis(meta_id[:, 0:1], axis=0), ys, None,
                                            compute_op=ALU.add).then_inc(S["scat"], 16)

            expert(0, 0, True)
            expert(1, 1, False)
            with pool.Fori(1, E // 2 - 1) as pair:
                expert(2 * pair, 0, False)
                expert(2 * pair + 1, 1, False)
            expert(E - 2, 0, False)
            expert(E - 1, 1, False, True)

        @block.scalar
        def _(act):
            def copy(dst, src):
                return nc.scalar.activation(dst, src, ACT.Copy)

            act.preload_act_table_set("natural_log_exp_and_others")
            act.wait_ge(S["consts"], 1)
            act.wait_ge(S["cin_k"], 16 * 5)

            def rstd(n, k):
                agg, ls, ys_ = ((S["ag"], S["lnv_s"], S["y0"]), (S["ag2"], S["lnv2"], S["y02"]))[k]
                act.wait_ge(agg, TT * (n + 1))
                nc.scalar.activation(lnv[:, k], mv[:, k, :, 1], ACT.Ln, bias=eps_t[:, 0:1]).then_inc(ls, 1)
                act.wait_ge(ls, n + 1)
                nc.scalar.activation(nt[:, k, 0], lnv[:, k], ACT.Exp, scale=-0.5).then_inc(ys_, 1)

            def xnT_copy(n, c, first):
                act.wait_ge(S["xnT_ps"], 2 * n + c + 1)
                if not first and c == 0:
                    act.wait_ge(S["qk_ps"], 4 * n)
                copy(xnT[:, c], M[1][:]).then_inc(S["xnT_sb"], 1)

            def part1(n, i, first, m=2):
                order = ORDER.index(i)
                act.wait_ge(S["qk_ps"], 4 * n + order + 1)
                if not first:
                    act.wait_ge(st_part[i], 48 * n)
                nc.scalar.activation(parts[:, i, 0, :], M[m][:], ACT.Identity, bias=bqk[:, i:i + 1]).then_inc(S["p1"], 1)

            def pv_copy(G, first=False):
                act.wait_ge(S["pv"], 4 * G + 4)
                if not first:
                    act.wait_ge(S["pvt"], G)
                copy(pvs[:], PV[:]).then_inc(S["pve"], 1)

            def attnT_copy(t, c, first):
                act.wait_ge(S["attnT_ps"], 2 * t + c + 1)
                if not first and c == 0:
                    act.wait_ge(S["o_ps"], 2 * t)
                copy(attnT[:, c], M[1][:]).then_inc(S["attnT_sb"], 1)

            def xn2T_copy(t, c, first):
                act.wait_ge(S["xn2T_ps"], 2 * t + c + 1)
                if not first and c == 0:
                    act.wait_ge(S["lgT_ps"], t)
                copy(xn2T[:, c], M[1][:]).then_inc(S["xn2T_sb"], 1)

            def lgT_copy(t, first):
                act.wait_ge(S["lgT_ps"], t + 1)
                if not first:
                    act.wait_ge(S["lg_ps"], t)
                copy(lgT[:], M[2][0:E, :]).then_inc(S["lgT_sb"], 1)

            def router_exp(t, first):
                act.wait_ge(S["rtc"], RT * t + 3)
                if not first:
                    act.wait_ge(S["cw_s"], t)
                nc.scalar.activation(rt[:, 1], rt[:, 0], ACT.Exp).then_inc(S["ex"], 1)

            def max_rows(G, g):
                act.wait_ge(S["neg"], 2 * G + 2)
                for c in range(2):
                    act.dma_start(qst[KS + c:KS + c + 1, g].rearrange("a h t -> a (h t)"),
                                  mneg[:, c, :]).then_inc(mrow[g], 16)

            def expert_high(e, c, first):
                if c == 0:
                    act.wait_ge(S["w_in"], 32 * (e + 1))
                    if not first:
                        act.wait_ge(S["wprep"], 16 * e)
                at = T * c + (2 * HID if c >= 4 else 0)
                a = wst[:, T * c:T * c + T]
                nc.scalar.activation(a, a, ACT.Copy, scale=WSC).then_inc(S["w_h"], 1)
                act.wait_ge(S["w_h"], 16 * e + 2 * c + 1)
                copy(wsh[:, at:at + T], a).then_inc(S["w_h"], 1)

            def batch(b, first, last):
                n, t = b + 1, b - 1
                second = isinstance(b, int) and b == 1

                def middle(s):
                    if s == 3 and not last:
                        xnT_copy(n, 1, False)
                    if s in (4, 5) and not first:
                        attnT_copy(t, s - 4, second)
                    if s == 9 and not first:
                        rstd(t, 1)
                    if s in (11, 12) and not first:
                        xn2T_copy(t, s - 11, second)

                def end(s):
                    if s == 2 and not last:
                        xnT_copy(n, 0, False)
                    if s in QK_STEPS and not last:
                        part1(n, ORDER[QK_STEPS.index(s)], False)
                    if s % 4 == 1 and not (last and s == 13):
                        max_rows(4 * b + s // 4 + 1, (s // 4 + 1) % 4)
                    if s == 12 and not first:
                        lgT_copy(t, second)
                    if s == 14 and not first:
                        router_exp(t, second)
                    if 4 <= s < 12:
                        expert_high(b, s - 4, first)

                for s in range(STEPS):
                    for j in range(4):
                        k = (16 * b + s) * 4 + j
                        act.wait_ge(S["b_done"], k + 1)
                        if j == 0 and not (first and s < 2):
                            act.wait_ge(S["pv"], 16 * b + s - 1)
                        nc.scalar.activation(pT[:, s % 2, j, :], Bp[:, j % 2, :], ACT.Exp).then_inc(S["exp"], 1)
                        if s == 1 and j == 0 and not last:
                            rstd(n, 0)
                        if j == 1:
                            middle(s)
                        if s % 4 == 0 and j == 2 and not (first and s == 0):
                            pv_copy(4 * b + s // 4 - 1, first=(first and s == 4))
                    end(s)

            rstd(0, 0)
            part1(0, 2, True, 2)
            part1(0, 3, True, 0)
            for c in range(KC):
                xnT_copy(0, c, True)
            part1(0, 0, True, 2)
            part1(0, 1, True, 0)
            max_rows(0, 0)

            batch(0, True, False)
            batch(1, False, False)
            with act.Fori(2, B - 1) as b:
                batch(b, False, False)
            batch(B - 1, False, True)
            t = B - 1
            pv_copy(4 * B - 1)
            attnT_copy(t, 0, False)
            attnT_copy(t, 1, False)
            rstd(t, 1)
            xn2T_copy(t, 0, False)
            xn2T_copy(t, 1, False)
            lgT_copy(t, False)
            router_exp(t, False)

            act.wait_ge(S["xn_s"], TT * B)
            nc.scalar.activation(warm[:], eps_t[:, 0:1], ACT.Gelu).then_inc(S["gelu"], 2)
            act.wait_ge(S["tabs"], 1)
            last = act.value_load(tab[0:1, 0, E:E + 1], min_val=8, max_val=MAXT)
            with act.Fori(0, last) as i:
                for k in range(2):
                    act.wait_ge(S["s1"], 2 * i + k + 1)
                    act.wait_ge(S["hl_s"], 2 * i + k + 1)
                    nc.scalar.activation(hf[:, T * k:T * k + T], A[:, k, :], ACT.Gelu,
                                         scale=1.0 / WSC).then_inc(S["gelu"], 1)

        @block.vector
        def _(dve):
            v = nc.vector

            def stats_of(src, n, k, tt, wait):
                if wait is not None:
                    dve.wait_ge(*wait)
                v.bn_stats(stats[:, k, tt], src[:, tt]).then_inc(S[("bn", "bn2")[k]], 1)

            def aggregate(n, k):
                for tt in range(TT):
                    wait(dve, S[("bn", "bn2")[k]], TT * n + tt + 1)
                    v.bn_aggr(mv[:, k, tt], stats[:, k, tt]).then_inc(S[("ag", "ag2")[k]], 1)

            def newton(n, k, step):
                y, a, b_, c_, r = (nt[:, k, m] for m in range(5))
                nw = S[("nw", "nw2")[k]]
                if step == 0:
                    dve.wait_ge(S[("y0", "y02")[k]], n + 1)
                    v.tensor_tensor(a, y, y, ALU.mult).then_inc(nw, 1)
                    return
                dve.wait_ge(nw, 4 * n + step)
                if step == 1:
                    v.scalar_tensor_tensor(b_, mv[:, k, :, 1], EPS, a, ALU.add, ALU.mult).then_inc(nw, 1)
                if step == 2:
                    v.tensor_scalar(c_, b_, -0.5, 1.5, ALU.mult, ALU.add).then_inc(nw, 1)
                if step == 3:
                    v.tensor_tensor(r, y, c_, ALU.mult).then_inc(nw, 1)

            def normalise(dst, src, n, k, wait):
                dve.wait_ge(S[("nw", "nw2")[k]], 4 * n + 4)
                if wait is not None:
                    dve.wait_ge(*wait)
                for tt in range(TT):
                    v.tensor_scalar(dst[:, tt], src[:, tt], mv[:, k, tt, 0:1], nt[:, k, 4, tt:tt + 1],
                                    ALU.subtract, ALU.mult).then_inc(S[("xn_s", "xn2_s")[k]], 1)

            def part_rest(n, i, first, m=2):
                order = ORDER.index(i)
                dve.wait_ge(S["p1"], 4 * n + order + 1)
                if not (first and order < 2):
                    dve.wait_ge(S["p3"], 4 * n + order - 1)
                v.scalar_tensor_tensor(rest[:, i % 2, :], M[m][:], bqk[:, i:i + 1], parts[:, i, 0, :],
                                       ALU.add, ALU.subtract).then_inc(S["r_s"], 1)

            def v_copy(n, h, first, m=2):
                dve.wait_ge(S["v_ps"], 2 * n + h + 1)
                if not first and h == 0:
                    dve.wait_ge(S["vaug_s"], 4 * n)
                v.tensor_tensor(vn[:, 2 * h:2 * h + 2], rows_of(m), bvb[:].rearrange("p (a d) -> p a d", a=1)
                                .to_broadcast([P, 2, D]), ALU.add).then_inc(S["v_sb"], 1)

            def reduce(b, h, j):
                k = (16 * b + h) * 4 + j
                dve.wait_ge(S["a_done"], k + 1)
                v.tensor_reduce(mx[:, (h // 4) % 2, h % 4, j:j + 1], A[:, j % 2, :], AX.X, ALU.max).then_inc(S["red"], 1)

            def negate(G):
                dve.wait_ge(S["maxT"], G + 1)
                v.tensor_scalar(mneg[:, 0, :], M[0][0:16, 0:P], -1.0, None, ALU.mult).then_inc(S["neg"], 1)
                dve.wait_ge(S["neg"], 2 * G + 1)
                v.scalar_tensor_tensor(mneg[:, 1, :], M[0][0:16, 0:P], -1.0, mneg[:, 0, :], ALU.mult,
                                       ALU.subtract).then_inc(S["neg"], 1)

            def attend(G, g, b, first):
                dve.wait_ge(S["pvt"], G + 1)
                v.reciprocal(rec[:], A4[:, :, :, DH]).then_inc(S["rec_s"], 1)
                dve.wait_ge(S["rec_s"], G + 1)
                if not first and g == 0:
                    dve.wait_ge(S["attnT_ps"], 2 * b)
                v.tensor_tensor(attn[:, :, 64 * g:64 * g + 64].rearrange("p q (j d) -> p q j d", j=4),
                                A4[:, :, :, 0:DH], rec[:].rearrange("p q (j a) -> p q j a", a=1)
                                .to_broadcast([P, TT, 4, DH]), ALU.mult).then_inc(S["attn_g"], 1)

            def add_residual(t, h, first):
                dve.wait_ge(S["o_ps"], 2 * t + h + 1)
                dve.wait_ge(S["xb"], t + 1)
                if not first and h == 0:
                    dve.wait_ge(S["x1_st"], 16 * t)
                v.tensor_tensor(x1[:, 2 * h:2 * h + 2], rows_of(2), xr[:, 2 * h:2 * h + 2], ALU.add).then_inc(S["x1_s"], 1)

            def bc(a):
                return a.rearrange("p (t a) -> p t a", a=1).to_broadcast([P, TT, E])

            def route(t, step):
                if step:
                    dve.wait_ge(S["rtc"], RT * t + step)
                if step == 0:
                    dve.wait_ge(S["lg_ps"], t + 1)
                    i_ = v.tensor_copy(lg[:], M[0][:, 0:TT * E].rearrange("p (t e) -> p t e", e=E))
                if step == 1:
                    i_ = v.tensor_reduce(sm[:, 0], lg[:], AX.X, ALU.max)
                if step == 2:
                    i_ = v.tensor_tensor(rt[:, 0], lg[:], bc(sm[:, 0]), ALU.subtract)
                if step == 3:
                    i_ = v.tensor_scalar(rt[:, 2], rt[:, 0], 0.0, float(E), ALU.is_lt, ALU.mult)
                if step == 4:
                    i_ = v.tensor_tensor(rt[:, 3], rt[:, 2], iota_e[:], ALU.add)
                if step == 5:
                    i_ = v.tensor_reduce(sm[:, 1], rt[:, 3], AX.X, ALU.min)
                if step == 6:
                    i_ = v.tensor_tensor(rt[:, 4], iota_e[:], bc(sm[:, 1]), ALU.is_equal)
                if step == 7:
                    i_ = v.scalar_tensor_tensor(rt[:, 5], rt[:, 4], -1e30, lg[:], ALU.mult, ALU.add)
                if step == 8:
                    i_ = v.tensor_reduce(sm[:, 2], rt[:, 5], AX.X, ALU.max)
                if step == 9:
                    i_ = v.tensor_tensor(rt[:, 6], rt[:, 5], bc(sm[:, 2]), ALU.subtract)
                if step == 10:
                    i_ = v.tensor_scalar(rt[:, 7], rt[:, 6], 0.0, float(E), ALU.is_lt, ALU.mult)
                if step == 11:
                    i_ = v.tensor_tensor(rt[:, 8], rt[:, 7], iota_e[:], ALU.add)
                if step == 12:
                    i_ = v.tensor_reduce(sm[:, 3], rt[:, 8], AX.X, ALU.min)
                if step == 13:
                    i_ = v.tensor_tensor(rt[:, 9], iota_e[:], bc(sm[:, 3]), ALU.is_equal)
                if step == 14:
                    i_ = v.tensor_tensor(mask[:], rt[:, 4], rt[:, 9], ALU.add)
                i_.then_inc(S["rtc"], 1)

            def weigh(t, step, first):
                if step:
                    dve.wait_ge(S["wgt"], (WT - 1) * t + step)
                if step == 0:
                    dve.wait_ge(S["ex"], t + 1)
                    i_ = v.tensor_reduce(sm[:, 4], rt[:, 1], AX.X, ALU.add)
                if step == 1:
                    i_ = v.reciprocal(sm[:, 5], sm[:, 4])
                if step == 2:
                    i_ = v.tensor_tensor(rt[:, 10], rt[:, 1], rt[:, 9], ALU.mult)
                if step == 3:
                    i_ = v.tensor_reduce(sm[:, 6], rt[:, 10], AX.X, ALU.add)
                if step == 4:
                    i_ = v.tensor_tensor(sm[:, 7], sm[:, 6], sm[:, 5], ALU.mult)
                if step == 5:
                    i_ = v.scalar_tensor_tensor(sm[:, 8], sm[:, 5], 1e-9, sm[:, 7], ALU.add, ALU.add)
                if step == 6:
                    i_ = v.reciprocal(sm[:, 9], sm[:, 8])
                if step == 7:
                    i_ = v.tensor_tensor(sm[:, 10], sm[:, 5], sm[:, 9], ALU.mult)
                if step == 8:
                    i_ = v.tensor_tensor(sm[:, 11], sm[:, 7], sm[:, 9], ALU.mult)
                if step == 9:
                    i_ = v.tensor_tensor(rt[:, 11], rt[:, 4], bc(sm[:, 10]), ALU.mult)
                if step == 10:
                    i_ = v.tensor_tensor(rt[:, 12], rt[:, 9], bc(sm[:, 11]), ALU.mult)
                if step == 11:
                    if not first:
                        dve.wait_ge(S["sct"], 128 * t)
                    v.tensor_tensor(row[:, :, W_CW:W_CW + E], rt[:, 11], rt[:, 12], ALU.add).then_inc(S["cw_s"], 1)
                    return
                i_.then_inc(S["wgt"], 1)

            def places(t, first):
                k = 0

                def link(i_):
                    nonlocal k
                    k += 1
                    i_.then_inc(S["tail_b"], 1)
                    dve.wait_ge(S["tail_b"], 6 * t + k)

                dve.wait_ge(S["rank_ps"], t + 1)
                C = M[0][:, 0:TT * E].rearrange("p (t e) -> p t e", e=E)
                link(v.tensor_tensor(rt[:, 10], C, base[:, 0:1].to_broadcast([P, TT, E]), ALU.add))
                link(v.tensor_tensor(base[:, 0], M[0][:, TT * E:TT * E + E], base[:, 0], ALU.add))
                link(v.tensor_tensor(rt[:, 11], rt[:, 10], region[:], ALU.add))
                v.tensor_tensor(rt[:, 12], rt[:, 11], rt[:, 4], ALU.mult)
                link(v.tensor_tensor(rt[:, 13], rt[:, 11], rt[:, 9], ALU.mult))
                link(v.tensor_reduce(slots[:], rt[:, 12:14].rearrange("p a t e -> p (a t) e"), AX.X, ALU.add))
                if not first:
                    dve.wait_ge(S["sct"], 128 * t)
                v.tensor_copy(slots_u[:], slots[:]).then_inc(S["slot"], 1)
                link(v.tensor_copy(base[:, 1], base[:, 0]))

            def batch(b, first, last):
                n, t = b + 1, b - 1
                second = isinstance(b, int) and b == 1

                def middle(s):
                    if s % 4 == 1 and not (last and s == 13):
                        negate(4 * b + s // 4 + 1)
                    if s == 2 and not first:
                        attend(4 * b - 1, 3, t, False)
                    if s == 6:
                        attend(4 * b, 0, b, first)
                    if s == 10:
                        attend(4 * b + 1, 1, b, first)
                    if s == 14:
                        attend(4 * b + 2, 2, b, first)

                def end(s):
                    if s == 1 and not last:
                        normalise(xn, xt, n, 0, (S["xnT_ps"], 2 * n))
                    if s in QK_STEPS and not last:
                        part_rest(n, ORDER[QK_STEPS.index(s)], False)
                    if s in (6, 7) and not first:
                        add_residual(t, s - 6, second)
                    if s in (8, 9) and not last:
                        v_copy(n, s - 8, False)
                    if s == 10 and not first:
                        normalise(xn2, x1, t, 1, None if second else (S["xl"], t))
                    if s == 13 and not first:
                        route(t, 0)
                    if s == 15 and not first:
                        places(t, second)

                for s in range(STEPS):
                    for j in range(4):
                        if not last or s + LEAD < STEPS:
                            reduce(b, s + LEAD, j)
                        if s == 0 and not last:
                            stats_of(xt, n, 0, j, (S["x_in"], 16 * (n + 1)) if j == 0 else None)
                            if j == 3:
                                aggregate(n, 0)
                        if s == 1 and not last:
                            newton(n, 0, j)
                        if s == 8 and not first:
                            stats_of(x1, t, 1, j, (S["x1_s"], 2 * t + 2) if j == 0 else None)
                        if s == 9 and j == 0 and not first:
                            aggregate(t, 1)
                        if s == 10 and not first:
                            newton(t, 1, j)
                        if s == 14 and not first:
                            for k in range(3):
                                route(t, 1 + 3 * j + k)
                        if s == 15 and not first:
                            for k in ((13, 14), (), (), ())[j]:
                                route(t, k)
                            for k in range((0, 0, 4, 8)[j], (0, 4, 8, WT)[j]):
                                weigh(t, k, second)
                        if j == 1:
                            middle(s)
                    end(s)

            for tt in range(TT):
                stats_of(xt, 0, 0, tt, (S["x_in"], 16))
            aggregate(0, 0)
            for k in range(4):
                newton(0, 0, k)
            normalise(xn, xt, 0, 0, None)
            dve.wait_ge(S["cin_k"], 16 * 5)
            dve.wait_ge(S["consts"], 1)
            dve.wait_ge(S["cin"], 16 * 6)
            for i, m in zip(ORDER, (2, 0, 2, 0)):
                part_rest(0, i, True, m)
            for h, m in enumerate((2, 0)):
                v_copy(0, h, True, m)
            for h in range(LEAD):
                for j in range(4):
                    reduce(0, h, j)
                if h == 3:
                    negate(0)

            batch(0, True, False)
            batch(1, False, False)
            with dve.Fori(2, B - 1) as b:
                batch(b, False, False)
            batch(B - 1, False, True)
            t = B - 1
            attend(4 * B - 1, 3, t, False)
            add_residual(t, 0, False)
            add_residual(t, 1, False)
            for j in range(TT):
                stats_of(x1, t, 1, j, (S["x1_s"], 2 * t + 2))
            aggregate(t, 1)
            for k in range(4):
                newton(t, 1, k)
            normalise(xn2, x1, t, 1, (S["xl"], t))
            for k in range(RT):
                route(t, k)
            for k in range(WT):
                weigh(t, k, False)
            places(t, False)

            kf = 0

            def link(i_):
                nonlocal kf
                kf += 1
                i_.then_inc(S["fin"], 1)
                dve.wait_ge(S["fin"], kf)

            link(v.tensor_copy(cnt_i[:, 0], base[:, 1]))
            link(v.tensor_scalar(cnt_f[:, 0], base[:, 1], float(P - 1), float(P), ALU.add, ALU.max))
            link(v.tensor_copy(cnt_i[:, 1], cnt_f[:, 0]))
            link(v.tensor_scalar(cnt_i[:, 2], cnt_i[:, 1], 7, None, ALU.logical_shift_right))
            link(v.tensor_copy(cnt_f[:, 1], cnt_i[:, 2]))
            link(v.memset(cnt_f[:, 0], 1.0))
            link(v.tensor_tensor_scan(cnt_f[:, 2], cnt_f[:, 0], cnt_f[:, 1], 0.0, ALU.mult, ALU.add))
            link(v.memset(tab[:, 0, 0:1], 0))
            link(v.tensor_copy(tab[:, 0, 1:E + 1], cnt_f[:, 2]))
            v.tensor_copy(tab[:, 1, 0:E], cnt_i[:, 0]).then_inc(S["tabs"], 1)

            def over_tiles(a):
                return a.rearrange("p (a e) -> p a e", a=1).to_broadcast([P, TN, E - 1])

            dve.wait_ge(S["w_l"], 2 * E)
            link(v.tensor_tensor(tt_f[:, 0], iota_t[:].rearrange("p (t a) -> p t a", a=1)
                                 .to_broadcast([P, TN, E - 1]), over_tiles(cnt_f[:, 2, 0:E - 1]), ALU.is_ge))
            link(v.tensor_tensor(tt_f[:, 1], tt_f[:, 0], over_tiles(cnt_f[:, 1, 0:E - 1]), ALU.mult))
            link(v.tensor_reduce(tt_s[:, 0:2], tt_f, AX.X, ALU.add))
            link(v.tensor_tensor(tt_s[:, 2], iota_t[:], tt_s[:, 1], ALU.subtract))
            link(v.tensor_scalar(tt_s[:, 3], tt_s[:, 2], float(P), None, ALU.mult))
            link(v.tensor_scalar(tt_s[:, 4], tt_s[:, 0], float(REGION), None, ALU.mult))
            link(v.tensor_tensor(tt_s[:, 5], tt_s[:, 3], tt_s[:, 4], ALU.add))
            link(v.scalar_tensor_tensor(tt_s[:, 6], iota_t[:], cnt_f[:, 2, E - 1:E], tt_s[:, 5],
                                        ALU.is_lt, ALU.mult))
            link(v.tensor_copy(tile_tab[:, 0], tt_s[:, 6]))
            v.tensor_copy(tile_tab[:, 1], tt_s[:, 0]).then_inc(S["tabs"], 1)

            dve.wait_ge(S["qk_ps"], 4 * B)
            v.memset(xT[:], 0.0).then_inc(S["xT_s"], 1)
            v.memset(hh, 0.0).then_inc(S["hh_s"], 2)
            v.memset(hl, 0.0).then_inc(S["hl_s"], 2)
            v.memset(ys, 0.0).then_inc(S["y_s"], 2)
            dve.wait_ge(S["xT_s"], 1)
            dve.wait_ge(S["hh_s"], 2)
            dve.wait_ge(S["hl_s"], 2)
            dve.wait_ge(S["tabs"], 1)
            last = dve.value_load(tab[0:1, 0, E:E + 1], min_val=8, max_val=MAXT)

            def xT_copy(i):
                dve.wait_ge(S["t_ps"], i + 1)
                v.tensor_copy(xT[:], XT16).then_inc(S["xT_s"], 1)

            def h_split(i, wait_s2):
                for k in range(2):
                    c = slice(T * k, T * k + T)
                    dve.wait_ge(S["gelu"], 2 * i + k + 3)
                    if wait_s2:
                        dve.wait_ge(S["s2"], i)
                    v.tensor_copy(hh[:, c], hf[:, c]).then_inc(S["hh_s"], 1)
                    dve.wait_ge(S["hh_s"], 2 * i + k + 3)
                    v.tensor_tensor(hl[:, c], hf[:, c], hh[:, c], ALU.subtract).then_inc(S["hl_s"], 1)

            def y_scale(i):
                dve.wait_ge(S["s2"], i + 1)
                dve.wait_ge(S["meta"], 32 * i + 32)
                dve.wait_ge(S["scat"], 16 * i + 16)
                v.tensor_copy(meta_id[:], meta_in[:]).then_inc(S["y_s"], 1)
                v.tensor_scalar(ys, PV[:, 0:D], meta_cw[:, 0:1], 1.0 / WSC, ALU.mult,
                                ALU.mult).then_inc(S["y_s"], 1)

            xT_copy(0)
            xT_copy(1)
            h_split(0, False)
            with dve.Fori(1, last) as i:
                xT_copy(i + 1)
                y_scale(i - 1)
                h_split(i, True)
            y_scale(last - 1)

        @block.tensor
        def _(pe):
            mm, tr = nc.tensor.matmul, nc.tensor.transpose
            pe.wait_ge(S["cin_k"], 16 * 5)

            def xnT_piece(n, c, after):
                pe.wait_ge(*after)
                pe.wait_ge(S["xn_s"], TT * (n + 1))
                for tt in range(TT):
                    i_ = tr(M[1][:, P * tt:P * tt + P], xn[:, tt, P * c:P * c + P], ident[:])
                i_.then_inc(S["xnT_ps"], 1)

            def qk_piece(n, i, after, m=2):
                if after is not None:
                    pe.wait_ge(*after)
                if i >= 2:
                    pe.wait_ge(S["ct_in"], 16 * (n + 1))
                else:
                    pe.wait_ge(S["xnT_sb"], 2 * n + 2)
                w, src = ((wq, xnT), (wk, ct))[i // 2]
                h = i % 2
                for c in range(KC):
                    i_ = mm(M[m][:], w[:, c, P * h:P * h + P], src[:, c, :], start=(c == 0), stop=(c == KC - 1))
                i_.then_inc(S["qk_ps"], 1)

            def v_piece(n, h, after, m=2):
                pe.wait_ge(*after)
                for q in range(2):
                    t_ = 2 * h + q
                    for c in range(KC):
                        i_ = mm(rows_of(m)[:, q], ct[:, c, P * t_:P * t_ + P], wv[:, c, :], start=(c == 0), stop=(c == KC - 1))
                i_.then_inc(S["v_ps"], 1)

            def max_piece(G, par, after):
                pe.wait_ge(*after)
                pe.wait_ge(S["red"], 16 * G + 16)
                tr(M[0][0:16, 0:P], mx[:, par].rearrange("p h t -> p (h t)"), ident[:]).then_inc(S["maxT"], 1)

            def pvt_piece(G, after):
                pe.wait_ge(*after)
                pe.wait_ge(S["pve"], G + 1)
                for q in range(TT):
                    i_ = tr(M[1][:, P * q:P * q + P], pvs[:, P * q:P * q + P], ident[:])
                i_.then_inc(S["pvt"], 1)

            def attnT_piece(t, c, after):
                pe.wait_ge(*after)
                pe.wait_ge(S["attn_g"], 4 * (t + 1))
                for tt in range(TT):
                    i_ = tr(M[1][:, P * tt:P * tt + P], attn[:, tt, P * c:P * c + P], ident[:])
                i_.then_inc(S["attnT_ps"], 1)

            def o_piece(t, h, after):
                pe.wait_ge(*after)
                pe.wait_ge(S["attnT_sb"], 2 * t + 2)
                for q in range(2):
                    t_ = 2 * h + q
                    for c in range(KC):
                        i_ = mm(rows_of(2)[:, q], attnT[:, c, P * t_:P * t_ + P], wo[:, c, :], start=(c == 0), stop=(c == KC - 1))
                i_.then_inc(S["o_ps"], 1)

            def xn2T_piece(t, c, after):
                pe.wait_ge(*after)
                pe.wait_ge(S["xn2_s"], TT * (t + 1))
                for tt in range(TT):
                    i_ = tr(M[1][:, P * tt:P * tt + P], xn2[:, tt, P * c:P * c + P], ident[:])
                i_.then_inc(S["xn2T_ps"], 1)

            def lgT_piece(t, after):
                pe.wait_ge(*after)
                pe.wait_ge(S["xn2T_sb"], 2 * t + 2)
                for c in range(KC):
                    i_ = mm(M[2][0:E, :], rw[:, c, :], xn2T[:, c, :], start=(c == 0), stop=(c == KC - 1))
                i_.then_inc(S["lgT_ps"], 1)

            def lg_piece(t, after):
                wait(pe, *after)
                wait(pe, S["lgT_sb"], t + 1)
                for tt in range(TT):
                    i_ = tr(M[0][:, E * tt:E * tt + E], lgT[:, P * tt:P * tt + P], ident[0:E, 0:E])
                i_.then_inc(S["lg_ps"], 1)

            def rank_piece(t):
                pe.wait_ge(S["rtc"], RT * (t + 1))
                mk = mask[:].rearrange("p t e -> p (t e)")
                mm(M[0][:, 0:TT * E], tri[:], mk, start=True, stop=False, skip_group_check=True)
                for k in range(1, TT):
                    mm(M[0][:, k * E:TT * E], ones[:], mk[:, 0:(TT - k) * E], start=False, stop=False, skip_group_check=True)
                for k in range(TT):
                    i_ = mm(M[0][:, TT * E:TT * E + E], ones[:], mk[:, k * E:k * E + E], start=False,
                            stop=(k == TT - 1), skip_group_check=True)
                i_.then_inc(S["rank_ps"], 1)

            def score_a(b, h, j):
                g = (h // 4) % 4
                if j == 0 and h % 4 == 0:
                    pe.wait_ge(qk_in[g], 96 * (b + 1 + h // 16))
                if not (isinstance(b, int) and b == 0 and h == 0 and j < 2):
                    pe.wait_ge(S["red"], (16 * b + h) * 4 + j - 1)
                mm(A[:, j % 2, :], qst[0:KS, g, h % 4, P * j:P * j + P], kst[0:KS, g, h % 4, :],
                   start=True, stop=True).then_inc(S["a_done"], 1)

            def score_b(b, s, j, first):
                g, kc = s // 4, s % 4
                if kc == 0 and j == 0:
                    pe.wait_ge(mrow[g], 32 * (b + 1))
                if not (first and s == 0 and j < 2):
                    pe.wait_ge(S["exp"], (16 * b + s) * 4 + j - 1)
                mm(Bp[:, j % 2, :], kst[0:KM, g, j, P * kc:P * kc + P], qst[0:KM, g, j, :],
                   start=True, stop=True).then_inc(S["b_done"], 1)

            def values(b, s, first):
                g, kc = (s // 4) % 4, s % 4
                pe.wait_ge(S["exp"], (16 * b + s) * 4 + 4)
                if kc == 0:
                    pe.wait_ge(S["vaug_s"], 4 * b + g + 1)
                    if not (first and s == 0):
                        pe.wait_ge(S["pve"], 4 * b + g)
                for j in range(4):
                    i_ = mm(PV[32 * j:32 * j + 32, :], vaug[:, g, kc, j, :], pT[:, s % 2, j, :],
                            start=(kc == 0), stop=(kc == 3))
                i_.then_inc(S["pv"], 1)

            def batch(b, first, last):
                n, t = b + 1, b - 1
                second = isinstance(b, int) and b == 1

                def middle(s):
                    if s % 4 == 1 and not (last and s == 13):
                        G = 4 * b + s // 4 + 1
                        after = (S["neg"], 2 * G) if s > 1 or first or second else (S["slot"], b - 1)
                        max_piece(G, (s // 4 + 1) % 2, after)
                    if s == 2 and not first:
                        pvt_piece(4 * b - 1, (S["attn_g"], 4 * b - 1))
                    if s == 3 and not last:
                        xnT_piece(n, 1, (S["xnT_sb"], 2 * n + 1))
                    if s == 4 and not first:
                        attnT_piece(t, 0, (S["attn_g"], 4 * b) if last else (S["xnT_sb"], 2 * n + 2))
                    if s == 5 and not first:
                        attnT_piece(t, 1, (S["attnT_sb"], 2 * t + 1))
                    if s == 6:
                        pvt_piece(4 * b, (S["xnT_sb"], 2 * n + 2) if first else (S["attnT_sb"], 2 * t + 2))
                    if s == 10:
                        pvt_piece(4 * b + 1, (S["attn_g"], 4 * b + 1))
                    if s == 11 and not first:
                        xn2T_piece(t, 0, (S["attn_g"], 4 * b + 2))
                    if s == 12 and not first:
                        xn2T_piece(t, 1, (S["xn2T_sb"], 2 * t + 1))
                    if s == 14:
                        pvt_piece(4 * b + 2, (S["attn_g"], 4 * b + 2) if first else (S["xn2T_sb"], 2 * t + 2))

                def end(s):
                    if s == 2 and not last:
                        xnT_piece(n, 0, (S["xnT_sb"], 2) if first else (S["attn_g"], 4 * b))
                    if s in QK_STEPS and not last:
                        k = QK_STEPS.index(s)
                        if k:
                            after = (S["r_s"], 4 * n + k)
                        else:
                            after = (S["v_sb"], 2 * b + 2) if first or second else (S["lgT_sb"], b - 1)
                        qk_piece(n, ORDER[k], after)
                    if s == 6 and not first:
                        o_piece(t, 0, (S["lgT_sb"], t) if last else (S["r_s"], 4 * n + 4))
                    if s == 7 and not first:
                        o_piece(t, 1, (S["x1_s"], 2 * t + 1))
                    if s == 8 and not last:
                        v_piece(n, 0, (S["r_s"], 4 * n + 4) if first else (S["x1_s"], 2 * t + 2))
                    if s == 9 and not last:
                        v_piece(n, 1, (S["v_sb"], 2 * n + 1))
                    if s == 12 and not first:
                        lgT_piece(t, (S["x1_s"], 2 * t + 2) if last else (S["v_sb"], 2 * n + 2))
                    if s == 13 and not first:
                        lg_piece(t, (S["neg"], 2 * (4 * b + 3) + 2) if last else (S["neg"], 2 * (4 * b + 4) + 2))
                    if s == 15 and not first:
                        rank_piece(t)

                for s in range(STEPS):
                    for j in range(4):
                        if not last or s + LEAD < STEPS:
                            score_a(b, s + LEAD, j)
                        score_b(b, s, j, first)
                        if j == 1:
                            middle(s)
                            if not (first and s == 0):
                                values(b, s - 1, first)
                    end(s)

            qk_piece(0, 2, None, 2)
            qk_piece(0, 3, None, 0)
            pe.wait_ge(S["consts"], 1)
            for c in range(KC):
                xnT_piece(0, c, (S["xn_s"], TT) if c == 0 else (S["xnT_sb"], 1))
            qk_piece(0, 0, (S["r_s"], 1), 2)
            qk_piece(0, 1, (S["r_s"], 2), 0)
            v_piece(0, 0, (S["r_s"], 3), 2)
            v_piece(0, 1, (S["r_s"], 4), 0)
            for h in range(LEAD):
                for j in range(4):
                    score_a(0, h, j)
                if h == 3:
                    max_piece(0, 0, (S["v_sb"], 2))

            batch(0, True, False)
            batch(1, False, False)
            with pe.Fori(2, B - 1) as b:
                batch(b, False, False)
            batch(B - 1, False, True)
            t = B - 1
            values(B, -1, False)
            pvt_piece(4 * B - 1, (S["attn_g"], 4 * B - 1))
            attnT_piece(t, 0, (S["attn_g"], 4 * B))
            attnT_piece(t, 1, (S["attnT_sb"], 2 * t + 1))
            o_piece(t, 0, (S["lgT_sb"], t))
            o_piece(t, 1, (S["x1_s"], 2 * t + 1))
            xn2T_piece(t, 0, (S["attnT_sb"], 2 * t + 2))
            xn2T_piece(t, 1, (S["xn2T_sb"], 2 * t + 1))
            lgT_piece(t, (S["x1_s"], 2 * t + 2))
            lg_piece(t, (S["slot"], t))
            rank_piece(t)

            def turn(i):
                pe.wait_ge(S["xrow_in"], 16 * i + 16)
                pe.wait_ge(S["xT_s"], i + 1)
                for c in range(4):
                    i_ = tr(XT16[:, P * c:P * c + P], xrow16[:, P * c:P * c + P], ident16[:])
                i_.then_inc(S["t_ps"], 1)

            def up(i, q):
                pe.wait_ge(S["xT_s"], i + 2)
                for k in range(2):
                    pe.wait_ge(S["gelu"], 2 * i + k + 1)
                    for m in range(4):
                        hc = 4 * k + m
                        terms = [(wp, c, xp) for c in range(KC) for wp, xp in ((0, 0), (0, 1), (1, 0))]
                        for z, (wp, c, xp) in enumerate(terms):
                            i_ = mm(A[:, k, P * m:P * m + P],
                                    whl[q][:, (2 * wp + c) * HID + P * hc:(2 * wp + c) * HID + P * hc + P],
                                    xT[:, (2 * xp + c) * P:(2 * xp + c) * P + P], start=(z == 0), stop=(z == 5))
                    i_.then_inc(S["s1"], 1)

            def down(i, q):
                pe.wait_ge(S["y_s"], 2 * i + 2)
                for k in range(2):
                    pe.wait_ge(S["hl_s"], 2 * i + k + 3)
                    for m in range(4):
                        hc = 4 * k + m
                        for z, (hp, wp) in enumerate(((hh, 0), (hh, 1), (hl, 0))):
                            at = (4 + 2 * wp) * HID + D * hc
                            i_ = mm(PV[:, 0:D], hp[:, P * hc:P * hc + P], whl[q][:, at:at + D],
                                    start=(hc == 0 and z == 0), stop=(hc == HC - 1 and z == 2))
                i_.then_inc(S["s2"], 1)

            pe.wait_ge(S["tabs"], 1)
            pe.wait_ge(S["pve"], 4 * B)
            pe.wait_ge(S["xn2T_sb"], 2 * B)
            pe.wait_ge(S["red"], 64 * B)

            def expert(pair, q, first):
                e = 2 * pair + q
                lo = pe.value_load(tab[0:1, 0, bass.ds(e, 1)], min_val=0, max_val=MAXT - 1)
                hi = pe.value_load(tab[0:1, 0, bass.ds(e + 1, 1)], min_val=1, max_val=MAXT)
                pe.wait_ge(wld[q], 16 * (pair + 1))
                up(lo, q)
                turn(lo + 1)
                if not first:
                    down(lo - 1, 1 - q)
                with pe.If(lo + 1 < hi):
                    with pe.Fori(lo + 1, hi) as i:
                        up(i, q)
                        turn(i + 1)
                        down(i - 1, q)
                with pe.Else():
                    pass

            turn(0)
            expert(0, 0, True)
            expert(0, 1, False)
            with pe.Fori(1, E // 2) as pair:
                expert(pair, 0, False)
                expert(pair, 1, False)
            last = pe.value_load(tab[0:1, 0, E:E + 1], min_val=8, max_val=MAXT)
            down(last - 1, 1)


RT = 15
WT = 12

_INS = ["x", "ctxT", "wqT", "wkT", "wvT", "woT", "bq", "bk", "bv", "bo", "rwT", "w1", "w2"]


def kernel(x, ctx_1024, L0_xattn_wq_w, L0_xattn_wq_b, L0_xattn_wk_w, L0_xattn_wk_b, L0_xattn_wv_w, L0_xattn_wv_b,
           L0_xattn_wo_w, L0_xattn_wo_b, L0_ffn_router_w, L0_ffn_w1, L0_ffn_w2):
    import numpy as np
    import concourse.bacc as bacc
    from concourse.bass_utils import run_bass_kernel_spmd

    arrays = {
        "x": x, "ctxT": np.transpose(np.asarray(ctx_1024), (0, 2, 1)),
        "wqT": np.asarray(L0_xattn_wq_w).T, "wkT": np.asarray(L0_xattn_wk_w).T,
        "wvT": np.asarray(L0_xattn_wv_w).T, "woT": np.asarray(L0_xattn_wo_w).T,
        "bq": L0_xattn_wq_b, "bk": L0_xattn_wk_b, "bv": L0_xattn_wv_b, "bo": L0_xattn_wo_b,
        "rwT": np.asarray(L0_ffn_router_w).T, "w1": L0_ffn_w1, "w2": L0_ffn_w2,
    }
    nc = bacc.Bacc("TRN2", target_bir_lowering=False, num_devices=1)
    ins, args = {}, []
    for name in _INS:
        a = np.ascontiguousarray(arrays[name])
        ins[f"in_{name}"] = a
        args.append(nc.dram_tensor(f"in_{name}", a.shape, mybir.dt.from_np(a.dtype), kind="ExternalInput").ap())
    out = nc.dram_tensor("out_rows", (N + P, D), F32, kind="ExternalOutput").ap()
    build(nc, *args, out)
    r = run_bass_kernel_spmd(nc, [ins], core_ids=[0])
    return r.results[0]["out_rows"][0:N].reshape(B, T, D)
```

```python
from contextlib import ExitStack

import concourse.bass as bass
from concourse import mybir

F32 = mybir.dt.float32
F16 = mybir.dt.float16
BF16 = mybir.dt.bfloat16
I32 = mybir.dt.int32
U32 = mybir.dt.uint32
ALU = mybir.AluOpType
ACT = mybir.ActivationFunctionType
AX = mybir.AxisListType

P = 128
B, T, D = 8, 512, 256
NH, DH = 16, 16
KC = D // P
TT = T // P
E, HID = 8, 1024
HC = HID // P
N = B * T
REGION = N + P
XW = D
W_CW, W_ID, ROWW = XW, XW + E, XW + E + 1
WSC = 256.0
PARTS = 3
RUNS = ((0, 48, 0, 3), (48, 32, 0, 2), (80, 16, 0, 1))
KRUNS = ((0, 48, 0, 3), (48, 32, 1, 3), (80, 16, 2, 3))
ORDER = (2, 3, 0, 1)
KS, KM = 96, 98
QK_STEPS = (1, 3, 6, 7)
REST_STEPS = (3, 4, 7, 9)
HIGH_STEPS = (3, 4, 5, 6, 7, 8, 9, 10)
STEPS = 16
LEAD = 6
EPS = 1e-5
MAXT = 2 * N // P + E
TN = MAXT + 3


def build(nc, x, ctxT, wqT, wkT, wvT, woT, bq, bk, bv, bo, rwT, w1, w2, out):
    scr = [nc.dram_tensor(f"scr_{n}", [B, NH, PARTS, DH, T], BF16).ap() for n in "qk"]
    wsp = nc.dram_tensor("wsp", [E, P, 8 * HID], F16).ap()
    rows_d = nc.dram_tensor("rows_d", [E * REGION, ROWW], F32).ap()

    with ExitStack() as ctx:
        def sb(name, shape, dt=F32):
            return ctx.enter_context(nc.sbuf_tensor(name, shape, dt))

        def ps(name, shape, dt=F32):
            return ctx.enter_context(nc.psum_tensor(name, shape, dt))

        def sem(name):
            return ctx.enter_context(nc.semaphore(name))

        ident = sb("ident", [P, P])
        ident16 = sb("ident16", [P, P], F16)
        tri = sb("tri", [P, P], BF16)
        ones = sb("ones", [P, P], BF16)
        iota_e = sb("iota_e", [P, TT, E])
        region = sb("region", [P, TT, E])
        tok_id = sb("tok_id", [P, B * TT], I32)
        pad_row = sb("pad_row", [P, ROWW])
        wq = sb("wq", [P, KC, D])
        wk = sb("wk", [P, KC, D])
        wv = sb("wv", [P, KC, D])
        wo = sb("wo", [P, KC, D])
        rw = sb("rw", [P, KC, E])
        bqk = sb("bqk", [P, 4])
        bvb = sb("bvb", [P, D])
        bob = sb("bob", [P, D])
        xt = sb("xt", [P, TT, D])
        xr = sb("xr", [P, TT, D])
        ct = sb("ct", [P, KC, T])
        xn = sb("xn", [P, TT, D])
        xnT = sb("xnT", [P, KC, T])
        parts = sb("parts", [P, 4, PARTS, T], BF16)
        rest = sb("rest", [P, 2, T])
        qst = sb("qst", [P, 4, 4, T], BF16)
        kst = sb("kst", [P, 4, 4, T], BF16)
        vn = sb("vn", [P, TT, D])
        vaug = sb("vaug", [P, 4, TT, 4, 32])
        pT = sb("pT", [P, 2, 4, T])
        pvs = sb("pvs", [P, T])
        attn = sb("attn", [P, TT, D])
        attnT = sb("attnT", [P, KC, T])
        x1 = sb("x1", [P, TT, D])
        xn2 = sb("xn2", [P, TT, D])
        xn2T = sb("xn2T", [P, KC, T])
        row = sb("row", [P, TT, ROWW])
        row16 = row[:, :, 0:XW].bitcast(F16)
        mx = sb("mx", [P, 2, 4, TT])
        mneg = sb("mneg", [16, 2, P], BF16)
        rec = sb("rec", [P, TT, 4])
        lgT = sb("lgT", [E, T])
        stats = sb("stats", [P, 2, TT, 6])
        mv = sb("mv", [P, 2, TT, 2])
        lnv = sb("lnv", [P, 2, TT])
        nt = sb("nt", [P, 2, 5, TT])
        eps_t = sb("eps_t", [P, 1])
        warm = sb("warm", [P, 1])
        lg = sb("lg", [P, TT, E])
        rt = sb("rt", [P, 14, TT, E])
        sm = sb("sm", [P, 12, TT])
        mask = sb("mask", [P, TT, E], BF16)
        base = sb("base", [P, 2, E])
        slots = sb("slots", [P, 2 * TT])
        slots_u = sb("slots_u", [P, 2 * TT], U32)
        cnt_i = sb("cnt_i", [P, 4, E], I32)
        cnt_f = sb("cnt_f", [P, 3, E])
        tab = sb("tab_tiles", [P, 2, E + 1], I32)
        wst = sb("wst", [P, 4 * HID])
        wsh = sb("wsh", [P, 8 * HID], F16)
        whl = [sb(f"whl{q}", [P, 8 * HID], F16) for q in range(2)]
        hf = xt[:].rearrange("p a b -> p (a b)")
        hh = xnT[:].rearrange("p a b -> p (a b)").bitcast(F16)[:, 0:HID]
        hl = xnT[:].rearrange("p a b -> p (a b)").bitcast(F16)[:, HID:2 * HID]
        xrow = sb("xrow", [P, XW])
        xrow2 = xn[:, 0]
        xrow16 = xrow2.bitcast(F16)
        xT = sb("xT", [P, 4 * P], F16)
        meta_cw = sb("meta_cw", [P, 1])
        meta_in = sb("meta_in", [P, 1], U32)
        meta_id = sb("meta_id", [P, 1], U32)
        iota_t = sb("iota_t", [P, TN])
        tt_f = wst[:, 0:2 * TN * (E - 1)].rearrange("p (a t e) -> p a t e", a=2, e=E - 1)
        tt_s = wst[:, 2 * HID:2 * HID + 7 * TN].rearrange("p (a t) -> p a t", a=7)
        tile_tab = sb("tile_tab", [P, 2, TN], I32)
        ys = pvs[:, 0:D]

        A = ps("A", [P, 2, T])
        Bp = ps("Bp", [P, 2, T])
        PV = ps("PV", [P, T])
        M = [ps(f"M{m}", [P, T]) for m in range(3)]

        names = """consts cin cin_k cin_q x_in xr_in ct_in bn ag lnv_s y0 nw xn_s xnT_ps xnT_sb qk_ps p1 r_s p2 p3
            v_ps v_sb vaug_s a_done red b_done exp pv pve pvt rec_s attn_g attnT_ps attnT_sb o_ps x1_s xb
            x1_st bn2 ag2 lnv2 y02 nw2 xn2_s xh xl xn2T_ps xn2T_sb lgT_ps lgT_sb lg_ps rtc ex cw_s rank_ps
            slot idw sct maxT neg fin ones_s kst_ones tabs padd w_s w_h w_l wprep xrow_in xrow_s t_ps xT_s
            s1 gelu hh_s hl_s s2 y_s meta scat ponce wgt plc passed""".split()
        S = {k: sem("s_" + k) for k in names}
        st_part = [sem(f"s_st{i}") for i in range(4)]
        qk_in = [sem(f"s_qk{g}") for g in range(4)]
        mrow = [sem(f"s_mrow{g}") for g in range(4)]
        w_in = [sem(f"s_w_in{k}") for k in range(2)]
        wld = [sem(f"s_wld{q}") for q in range(2)]

        def wait(eng, s, value):
            eng.wait_ge(s, value)
            if not isinstance(value, int):
                eng.sem_inc(S["passed"], 1)

        def pad(eng, e):
            c = eng.value_load(tab[0:1, 1, e:e + 1], min_val=0, max_val=N)
            eng.dma_start(rows_d[bass.ds(c + e * REGION, P)], pad_row[:]).then_inc(S["padd"], 16)

        A4 = M[1][:].rearrange("p (q j r) -> p q j r", q=TT, j=4)
        XT16 = M[1][:].bitcast(F16)[:, 0:4 * P]

        def rows_of(m):
            return M[m][:].rearrange("p (a n) -> p a n", a=2)

        block = ctx.enter_context(nc.Block())

        @block.sync
        def _(sp):
            def load_w(w, src, sem_):
                sp.dma_start(w[:], src.rearrange("(c p) n -> p c n", p=P)).then_inc(sem_, 16)

            def load_x(b):
                sp.dma_start(xt[:], x[bass.ds(b, 1)].rearrange("a (t p) d -> p (a t) d", p=P)).then_inc(S["x_in"], 16)

            def load_ct(b):
                sp.dma_start(ct[:], ctxT[bass.ds(b, 1)].rearrange("a (c p) t -> p (a c) t", p=P)).then_inc(S["ct_in"], 16)

            def store_parts(n, i):
                dst, h = scr[i // 2], i % 2
                for c in range(PARTS):
                    wait(sp, (S["p1"], S["p2"], S["p3"])[c], 4 * n + ORDER.index(i) + 1)
                    at = c if i < 2 else PARTS - 1 - c
                    sp.dma_start(dst[bass.ds(n, 1), 8 * h:8 * h + 8, at].rearrange("a h d t -> (a h) d t"),
                                 parts[:, i, c, :]).then_inc(st_part[i], 16)

            def load_stack(n, g, first, which=(0, 1)):
                for i in which:
                    wait(sp, st_part[2 * i + g // 2], 48 * (n + 1))
                if not first:
                    wait(sp, S["b_done"], 64 * (n - 1) + 16 * (g + 1))
                for i in which:
                    st, src, runs = ((qst, scr[0], RUNS), (kst, scr[1], KRUNS))[i]
                    for r0, nr, c0, c1 in runs:
                        sp.dma_start(st[r0:r0 + nr, g],
                                     src[bass.ds(n, 1), 4 * g:4 * g + 4, c0:c1].rearrange("a h c d t -> (c d) (a h) t")
                                     ).then_inc(qk_in[g], 16)

            def store_x1(t):
                wait(sp, S["x1_s"], 2 * t + 2)
                sp.dma_start(out[bass.ds(t * T, T)].rearrange("(t p) d -> p t d", p=P), x1[:]).then_inc(S["x1_st"], 16)

            def load_xr(t, first):
                if not first:
                    wait(sp, S["x1_s"], 2 * t)
                sp.dma_start(xr[:], x[bass.ds(t, 1)].rearrange("a (t p) d -> p (a t) d", p=P)).then_inc(S["xr_in"], 16)

            def prep(e, k, first):
                if not first:
                    wait(sp, S["w_l"], 2 * e - 1 + k)
                src = (w1, w2)[k][bass.ds(e, 1)].rearrange("a (c p) n -> p (a c) n", p=P)
                sp.dma_start(wst[:, 2 * HID * k:2 * HID * k + 2 * HID].rearrange("p (c n) -> p c n", c=(KC, HC)[k]),
                             src).then_inc(w_in[k], 16)

            def prep_out(e, k):
                wait(sp, S["w_l"], 2 * e + k + 1)
                c = slice(4 * HID * k, 4 * HID * k + 4 * HID)
                sp.dma_start(wsp[bass.ds(e, 1), :, c].rearrange("a p n -> p (a n)"), wsh[:, c]).then_inc(S["wprep"], 16)

            load_w(wk, wkT, S["cin_k"])
            load_ct(0)
            for i, bias in enumerate((bk, bq)):
                sp.dma_start(bqk[:, 2 - 2 * i:4 - 2 * i], bias.rearrange("(h p) -> p h", p=P),
                             allow_slow_non_contiguous=True).then_inc(S["cin_k"], 16)
            load_w(wv, wvT, S["cin"])
            for t_, bias in ((bvb, bv), (bob, bo)):
                sp.dma_start(t_[:], bias.rearrange("(a n) -> a n", a=1).to_broadcast([P, D])).then_inc(S["cin"], 16)
            load_w(wo, woT, S["cin"])
            load_w(rw, rwT, S["cin"])
            for i in ORDER[:2]:
                store_parts(0, i)
            load_stack(0, 0, True, (1,))
            store_parts(0, ORDER[2])
            load_stack(0, 0, True, (0,))
            store_parts(0, ORDER[3])
            wait(sp, S["xn_s"], TT)
            load_x(1)
            wait(sp, S["v_ps"], 2)
            load_ct(1)
            for g in range(1, 4):
                load_stack(0, g, True)

            def batch(b, first, last):
                n, t = b + 1, b - 1
                if not first:
                    load_stack(b, 3, False)
                prep(b, 0, first)
                if not last:
                    for i in ORDER[:2]:
                        store_parts(n, i)
                    wait(sp, S["xn_s"], TT * (n + 1))
                    load_x((b + 2) % B)
                prep(b, 1, first)
                if not first:
                    store_x1(t)
                load_xr(b, first)
                if not last:
                    load_stack(n, 0, False, (1,))
                    store_parts(n, ORDER[2])
                    load_stack(n, 0, False, (0,))
                    store_parts(n, ORDER[3])
                    load_stack(n, 1, False)
                prep_out(b, 0)
                if not last:
                    load_stack(n, 2, False)
                    wait(sp, S["v_ps"], 2 * (n + 1))
                    load_ct((b + 2) % B)
                prep_out(b, 1)

            batch(0, True, False)
            batch(1, False, False)
            with sp.Fori(2, B - 1) as b:
                batch(b, False, False)
            batch(B - 1, False, True)
            store_x1(B - 1)

            wait(sp, S["tabs"], 1)
            for e in range(E // 2):
                pad(sp, e)
            wait(sp, S["tabs"], 2)

            def row_at(i):
                return sp.value_load(tile_tab[0:1, 0, bass.ds(i, 1)], min_val=0, max_val=E * REGION - P)

            def load_row(i, at):
                if not isinstance(i, int) or i:
                    wait(sp, S["xrow_s"], i)
                sp.dma_start(xrow[:], rows_d[bass.ds(at, P), 0:XW]).then_inc(S["xrow_in"], 16)

            def load_meta(i):
                at = row_at(i)
                e = sp.value_load(tile_tab[0:1, 1, bass.ds(i, 1)], min_val=0, max_val=E - 1)
                wait(sp, S["y_s"], 2 * i + 2)
                sp.dma_start(meta_cw[:], rows_d[bass.ds(at, P), bass.ds(e + W_CW, 1)],
                             allow_slow_non_contiguous=True).then_inc(S["meta"], 16)
                sp.dma_start(meta_in[:], rows_d[bass.ds(at, P), W_ID:W_ID + 1].bitcast(U32),
                             allow_slow_non_contiguous=True).then_inc(S["meta"], 16)

            at0, at1, at2 = (row_at(i) for i in range(3))
            last = sp.value_load(tab[0:1, 0, E:E + 1], min_val=8, max_val=MAXT)
            wait(sp, S["padd"], 16 * E)
            wait(sp, S["sct"], 16 * 2 * TT * B)
            load_row(0, at0)
            load_row(1, at1)
            load_row(2, at2)
            with sp.Fori(0, last) as i:
                load_row(i + 3, row_at(i + 3))
                load_meta(i)
            wait(sp, S["xrow_in"], last * 16 + 48)
            wait(sp, S["scat"], last * 16 + 16)

        @block.gpsimd
        def _(pool):
            def once(instr, k):
                instr.then_inc(S["ponce"], 1)
                wait(pool, S["ponce"], k)

            once(nc.gpsimd.memset(ident[:], 0.0), 1)
            once(nc.gpsimd.affine_select(out=ident[:], in_=ident[:], compare_op=ALU.not_equal, fill=1.0, base=0,
                                         pattern=[[-1, P]], channel_multiplier=1), 2)
            once(nc.gpsimd.tensor_copy(ident16[:], ident[:]), 3)
            once(nc.gpsimd.memset(eps_t[:], EPS), 4)
            once(nc.gpsimd.memset(ones[:], 1.0), 5)
            once(nc.gpsimd.affine_select(out=tri[:], in_=ones[:], compare_op=ALU.is_ge, fill=0.0, base=-1,
                                         pattern=[[1, P]], channel_multiplier=-1), 6)
            wait(pool, S["cin_q"], 16)
            once(nc.gpsimd.tensor_scalar(wq[:], wq[:], DH ** -0.5, None, ALU.mult), 7)
            wait(pool, S["cin_k"], 16 * 3)
            nc.gpsimd.tensor_scalar(bqk[:, 0:2], bqk[:, 0:2], DH ** -0.5, None, ALU.mult).then_inc(S["consts"], 1)
            once(nc.gpsimd.iota(iota_e[:], [[0, TT], [1, E]], base=0, channel_multiplier=0,
                                allow_small_or_imprecise_dtypes=True), 8)
            once(nc.gpsimd.iota(tok_id[:], [[P, B * TT]], base=0, channel_multiplier=1), 9)
            once(nc.gpsimd.memset(pad_row[:], 0.0), 10)
            once(nc.gpsimd.iota(pad_row[:, W_ID:W_ID + 1].bitcast(I32), [[1, 1]], base=N, channel_multiplier=1), 11)
            once(nc.gpsimd.memset(base[:], 0.0), 12)
            once(nc.gpsimd.tensor_scalar(region[:], iota_e[:], float(REGION), None, ALU.mult), 13)
            once(nc.gpsimd.iota(iota_t[:], [[1, TN]], base=0, channel_multiplier=0,
                                allow_small_or_imprecise_dtypes=True), 14)
            pool.dma_start(out[N:N + P], pad_row[:, 0:D]).then_inc(S["scat"], 16)

            def split(n, i, first):
                k = 4 * n + ORDER.index(i) + 1
                wait(pool, S["r_s"], k)
                if not first:
                    wait(pool, st_part[i], 48 * n)
                nc.gpsimd.tensor_copy(parts[:, i, 1, :], rest[:, i % 2, :]).then_inc(S["p2"], 1)
                wait(pool, S["p2"], k)
                nc.gpsimd.tensor_tensor(parts[:, i, 2, :], rest[:, i % 2, :], parts[:, i, 1, :],
                                        ALU.subtract).then_inc(S["p3"], 1)

            def values(n, g, first):
                wait(pool, S["v_sb"], 2 * n + 2)
                if not first:
                    wait(pool, S["pv"], 16 * (n - 1) + 4 * (g + 1))
                c = slice(4 * DH * g, 4 * DH * g + 4 * DH)
                nc.gpsimd.tensor_tensor(vaug[:, g, :, :, 0:DH], vn[:, :, c].rearrange("p t (h d) -> p t h d", h=4),
                                        bvb[:, c].rearrange("p (a h d) -> p a h d", a=1, h=4)
                                        .to_broadcast([P, TT, 4, DH]), ALU.add).then_inc(S["vaug_s"], 1)

            def expert_low(e, k):
                wait(pool, S["w_h"], 8 * e + 4 * k + 4)
                a, hi, lo = wst[:, 2 * HID * k:2 * HID * k + 2 * HID], 4 * HID * k, 4 * HID * k + 2 * HID
                nc.gpsimd.tensor_scalar(a, a, WSC, None, ALU.mult).then_inc(S["w_s"], 1)
                wait(pool, S["w_s"], 2 * e + k + 1)
                nc.gpsimd.tensor_tensor(wsh[:, lo:lo + 2 * HID], a, wsh[:, hi:hi + 2 * HID],
                                        ALU.subtract).then_inc(S["w_l"], 1)

            def residual(t):
                wait(pool, S["xr_in"], 16 * (t + 1))
                nc.gpsimd.tensor_tensor(xr[:], xr[:], bob[:].rearrange("p (a d) -> p a d", a=1).to_broadcast([P, TT, D]),
                                        ALU.add).then_inc(S["xb"], 1)

            def rows(t, first):
                wait(pool, S["xn2_s"], TT * (t + 1))
                if not first:
                    wait(pool, S["sct"], 128 * t)
                nc.gpsimd.tensor_copy(row16[:, :, 0:D], xn2[:]).then_inc(S["xh"], 1)
                wait(pool, S["xh"], t + 1)
                nc.gpsimd.tensor_tensor(row16[:, :, D:2 * D], xn2[:], row16[:, :, 0:D], ALU.subtract).then_inc(S["xl"], 1)
                nc.gpsimd.tensor_copy(row[:, :, W_ID].bitcast(I32), tok_id[:, bass.ds(t * TT, TT)]).then_inc(S["idw"], 1)

            def scatter(t):
                wait(pool, S["slot"], t + 1)
                wait(pool, S["cw_s"], t + 1)
                wait(pool, S["xl"], t + 1)
                wait(pool, S["idw"], t + 1)
                for c in range(2):
                    for tt in range(TT):
                        pool.indirect_dma_start(
                            rows_d, bass.IndirectOffsetOnAxis(slots_u[:, c * TT + tt:c * TT + tt + 1], axis=0),
                            row[:, tt, :], None).then_inc(S["sct"], 16)

            for i in ORDER:
                split(0, i, True)
            wait(pool, S["cin"], 16 * 5)
            wait(pool, S["ones_s"], 1)
            for g in range(4):
                values(0, g, True)

            def batch(b, first, last):
                n, t = b + 1, b - 1
                if not first:
                    values(b, 3, False)
                if not last:
                    for i in ORDER:
                        split(n, i, False)
                if not first:
                    wait(pool, S["wprep"], 32 * b)
                expert_low(b, 0)
                if not first:
                    rows(t, first=(isinstance(b, int) and b == 1))
                expert_low(b, 1)
                if not last:
                    for g in range(3):
                        values(n, g, False)
                residual(b)
                if not first:
                    scatter(t)

            batch(0, True, False)
            batch(1, False, False)
            with pool.Fori(2, B - 1) as b:
                batch(b, False, False)
            batch(B - 1, False, True)

            def load_weights(e, q):
                pool.dma_start(whl[q][:], wsp[bass.ds(e, 1)].rearrange("a p n -> p (a n)")).then_inc(wld[q], 16)

            load_weights(0, 0)
            load_weights(1, 1)
            rows(B - 1, False)
            scatter(B - 1)

            wait(pool, S["wprep"], 32 * E)
            wait(pool, S["tabs"], 1)
            wait(pool, S["x1_st"], 16 * B)

            def expert(e, q, first, last=False):
                lo = pool.value_load(tab[0:1, 0, bass.ds(e, 1)], min_val=0, max_val=MAXT - 1)
                hi = pool.value_load(tab[0:1, 0, bass.ds(e + 1, 1)], min_val=1, max_val=MAXT)
                if not first and not last:
                    wait(pool, S["s2"], lo)
                    load_weights(e + 1, 1 - q)
                with pool.Fori(lo, hi) as i:
                    wait(pool, S["y_s"], 2 * i + 4)
                    pool.indirect_dma_start(out, bass.IndirectOffsetOnAxis(meta_id[:, 0:1], axis=0), ys, None,
                                            compute_op=ALU.add).then_inc(S["scat"], 16)

            expert(0, 0, True)
            expert(1, 1, False)
            with pool.Fori(1, E // 2 - 1) as pair:
                expert(2 * pair, 0, False)
                expert(2 * pair + 1, 1, False)
            expert(E - 2, 0, False)
            expert(E - 1, 1, False, True)

        @block.scalar
        def _(act):
            def copy(dst, src):
                return nc.scalar.activation(dst, src, ACT.Copy)

            act.dma_start(xt[:], x[0:1].rearrange("a (t p) d -> p (a t) d", p=P)).then_inc(S["x_in"], 16)
            act.dma_start(wq[:], wqT.rearrange("(c p) n -> p c n", p=P)).then_inc(S["cin_q"], 16)
            act.preload_act_table_set("natural_log_exp_and_others")
            act.wait_ge(S["ponce"], 4)
            act.wait_ge(S["cin_k"], 16 * 3)

            def rstd(n, k):
                agg, ls, ys_ = ((S["ag"], S["lnv_s"], S["y0"]), (S["ag2"], S["lnv2"], S["y02"]))[k]
                act.wait_ge(agg, TT * (n + 1))
                nc.scalar.activation(lnv[:, k], mv[:, k, :, 1], ACT.Ln, bias=eps_t[:, 0:1]).then_inc(ls, 1)
                act.wait_ge(ls, n + 1)
                nc.scalar.activation(nt[:, k, 0], lnv[:, k], ACT.Exp, scale=-0.5).then_inc(ys_, 1)

            def xnT_copy(n, c, first):
                act.wait_ge(S["xnT_ps"], 2 * n + c + 1)
                if not first and c == 0:
                    act.wait_ge(S["qk_ps"], 4 * n)
                copy(xnT[:, c], M[1][:]).then_inc(S["xnT_sb"], 1)

            def part1(n, i, first, m=2):
                order = ORDER.index(i)
                act.wait_ge(S["qk_ps"], 4 * n + order + 1)
                if not first:
                    act.wait_ge(st_part[i], 48 * n)
                nc.scalar.activation(parts[:, i, 0, :], M[m][:], ACT.Identity, bias=bqk[:, i:i + 1]).then_inc(S["p1"], 1)

            def v_copy(n, h, first, m=2):
                act.wait_ge(S["v_ps"], 2 * n + h + 1)
                if not first and h == 0:
                    act.wait_ge(S["vaug_s"], 4 * n)
                copy(vn[:, 2 * h:2 * h + 2], rows_of(m)).then_inc(S["v_sb"], 1)

            def pv_copy(G, first=False):
                act.wait_ge(S["pv"], 4 * G + 4)
                if not first:
                    act.wait_ge(S["pvt"], G)
                copy(pvs[:], PV[:]).then_inc(S["pve"], 1)

            def attnT_copy(t, c, first):
                act.wait_ge(S["attnT_ps"], 2 * t + c + 1)
                if not first and c == 0:
                    act.wait_ge(S["o_ps"], 2 * t)
                copy(attnT[:, c], M[1][:]).then_inc(S["attnT_sb"], 1)

            def xn2T_copy(t, c, first):
                act.wait_ge(S["xn2T_ps"], 2 * t + c + 1)
                if not first and c == 0:
                    act.wait_ge(S["lgT_ps"], t)
                copy(xn2T[:, c], M[1][:]).then_inc(S["xn2T_sb"], 1)

            def lgT_copy(t, first):
                act.wait_ge(S["lgT_ps"], t + 1)
                if not first:
                    act.wait_ge(S["lg_ps"], t)
                copy(lgT[:], M[2][0:E, :]).then_inc(S["lgT_sb"], 1)

            def router_exp(t, first):
                act.wait_ge(S["rtc"], RT * t + 3)
                if not first:
                    act.wait_ge(S["cw_s"], t)
                nc.scalar.activation(rt[:, 1], rt[:, 0], ACT.Exp).then_inc(S["ex"], 1)

            def max_rows(G, g):
                act.wait_ge(S["neg"], 2 * G + 2)
                for c in range(2):
                    act.dma_start(qst[KS + c:KS + c + 1, g].rearrange("a h t -> a (h t)"),
                                  mneg[:, c, :]).then_inc(mrow[g], 16)

            def expert_high(e, c, first):
                if c % 4 == 0:
                    act.wait_ge(w_in[c // 4], 16 * (e + 1))
                if c == 0 and not first:
                    act.wait_ge(S["wprep"], 32 * e)
                at = T * c + (2 * HID if c >= 4 else 0)
                a = wst[:, T * c:T * c + T]
                nc.scalar.activation(wsh[:, at:at + T], a, ACT.Copy, scale=WSC).then_inc(S["w_h"], 1)

            def batch(b, first, last):
                n, t = b + 1, b - 1
                second = isinstance(b, int) and b == 1

                def middle(s):
                    if s == 2 and not last:
                        rstd(n, 0)
                    if s == 3 and not first:
                        attnT_copy(t, 0, second)
                    if s in (4, 5) and not last:
                        xnT_copy(n, s - 4, False)
                    if s == 7 and not first:
                        rstd(t, 1)
                    if s == 9 and not first:
                        xn2T_copy(t, 0, second)
                    if s == 10 and not first:
                        lgT_copy(t, second)

                def end(s):
                    if s in HIGH_STEPS:
                        expert_high(b, HIGH_STEPS.index(s), first)
                    if s in QK_STEPS and not last:
                        part1(n, ORDER[QK_STEPS.index(s)], False)
                    if s == 3 and not first:
                        attnT_copy(t, 1, second)
                    if s % 4 == 2 and not (last and s == 14):
                        max_rows(4 * b + s // 4 + 1, (s // 4 + 1) % 4)
                    if s == 9 and not first:
                        xn2T_copy(t, 1, second)
                    if s == 11 and not first:
                        router_exp(t, second)
                    if s in (14, 15) and not last:
                        v_copy(n, s - 14, False)
                for s in range(STEPS):
                    for j in range(4):
                        k = (16 * b + s) * 4 + j
                        act.wait_ge(S["b_done"], k + 1)
                        if j == 0 and not (first and s < 2):
                            act.wait_ge(S["pv"], 16 * b + s - 1)
                        nc.scalar.activation(pT[:, s % 2, j, :], Bp[:, j % 2, :], ACT.Exp).then_inc(S["exp"], 1)
                        if j == 1:
                            middle(s)
                        if s % 4 == 0 and j == 2 and not (first and s == 0):
                            pv_copy(4 * b + s // 4 - 1, first=(first and s == 4))
                    end(s)

            rstd(0, 0)
            part1(0, 2, True, 2)
            for c in range(KC):
                xnT_copy(0, c, True)
            part1(0, 3, True, 0)
            act.wait_ge(S["consts"], 1)
            part1(0, 0, True, 2)
            part1(0, 1, True, 0)
            v_copy(0, 0, True, 2)
            v_copy(0, 1, True, 0)
            act.wait_ge(S["ponce"], 5)
            for g in range(4):
                copy(kst[KS:KM, g].rearrange("p h (a n) -> p (h a) n", n=P),
                     ones[KS:KM, :].rearrange("p (a n) -> p a n", a=1).to_broadcast([KM - KS, 4 * TT, P])
                     ).then_inc(S["kst_ones"], 1)
            max_rows(0, 0)

            batch(0, True, False)
            batch(1, False, False)
            with act.Fori(2, B - 1) as b:
                batch(b, False, False)
            batch(B - 1, False, True)
            t = B - 1
            pv_copy(4 * B - 1)
            attnT_copy(t, 0, False)
            attnT_copy(t, 1, False)
            rstd(t, 1)
            xn2T_copy(t, 0, False)
            xn2T_copy(t, 1, False)
            lgT_copy(t, False)
            router_exp(t, False)

            act.wait_ge(S["xn_s"], TT * B)
            act.wait_ge(S["xnT_ps"], 2 * B)
            nc.scalar.activation(warm[:], eps_t[:, 0:1], ACT.Gelu).then_inc(S["gelu"], 2)
            act.wait_ge(S["tabs"], 1)
            for e in range(E // 2, E):
                pad(act, e)
            last = act.value_load(tab[0:1, 0, E:E + 1], min_val=8, max_val=MAXT)

            def row_copy(i):
                act.wait_ge(S["xrow_in"], 16 * i + 16)
                if not isinstance(i, int) or i:
                    act.wait_ge(S["t_ps"], i)
                copy(xrow2, xrow[:]).then_inc(S["xrow_s"], 1)

            row_copy(0)
            row_copy(1)
            with act.Fori(0, last) as i:
                for k in range(2):
                    act.wait_ge(S["s1"], 2 * i + k + 1)
                    act.wait_ge(S["hl_s"], 2 * i + k + 1)
                    nc.scalar.activation(hf[:, T * k:T * k + T], A[:, k, :], ACT.Gelu,
                                         scale=1.0 / WSC).then_inc(S["gelu"], 1)
                row_copy(i + 2)

        @block.vector
        def _(dve):
            v = nc.vector

            def stats_of(src, n, k, tt, wait):
                if wait is not None:
                    dve.wait_ge(*wait)
                v.bn_stats(stats[:, k, tt], src[:, tt]).then_inc(S[("bn", "bn2")[k]], 1)

            def aggregate(n, k):
                for tt in range(TT):
                    wait(dve, S[("bn", "bn2")[k]], TT * n + tt + 1)
                    v.bn_aggr(mv[:, k, tt], stats[:, k, tt]).then_inc(S[("ag", "ag2")[k]], 1)

            def newton(n, k, step):
                y, a, b_, c_, r = (nt[:, k, m] for m in range(5))
                nw = S[("nw", "nw2")[k]]
                if step == 0:
                    dve.wait_ge(S[("y0", "y02")[k]], n + 1)
                    v.tensor_tensor(a, y, y, ALU.mult).then_inc(nw, 1)
                    return
                dve.wait_ge(nw, 4 * n + step)
                if step == 1:
                    v.scalar_tensor_tensor(b_, mv[:, k, :, 1], EPS, a, ALU.add, ALU.mult).then_inc(nw, 1)
                if step == 2:
                    v.tensor_scalar(c_, b_, -0.5, 1.5, ALU.mult, ALU.add).then_inc(nw, 1)
                if step == 3:
                    v.tensor_tensor(r, y, c_, ALU.mult).then_inc(nw, 1)

            def normalise(dst, src, n, k, wait):
                dve.wait_ge(S[("nw", "nw2")[k]], 4 * n + 4)
                if wait is not None:
                    dve.wait_ge(*wait)
                for tt in range(TT):
                    v.tensor_scalar(dst[:, tt], src[:, tt], mv[:, k, tt, 0:1], nt[:, k, 4, tt:tt + 1],
                                    ALU.subtract, ALU.mult).then_inc(S[("xn_s", "xn2_s")[k]], 1)

            def part_rest(n, i, first, m=2):
                order = ORDER.index(i)
                dve.wait_ge(S["p1"], 4 * n + order + 1)
                if not (first and order < 2):
                    dve.wait_ge(S["p3"], 4 * n + order - 1)
                v.scalar_tensor_tensor(rest[:, i % 2, :], M[m][:], bqk[:, i:i + 1], parts[:, i, 0, :],
                                       ALU.add, ALU.subtract).then_inc(S["r_s"], 1)

            def reduce(b, h, j):
                k = (16 * b + h) * 4 + j
                dve.wait_ge(S["a_done"], k + 1)
                v.tensor_reduce(mx[:, (h // 4) % 2, h % 4, j:j + 1], A[:, j % 2, :], AX.X, ALU.max).then_inc(S["red"], 1)

            def negate(G):
                dve.wait_ge(S["maxT"], G + 1)
                v.tensor_scalar(mneg[:, 0, :], M[0][0:16, 0:P], -1.0, None, ALU.mult).then_inc(S["neg"], 1)
                dve.wait_ge(S["neg"], 2 * G + 1)
                v.scalar_tensor_tensor(mneg[:, 1, :], M[0][0:16, 0:P], -1.0, mneg[:, 0, :], ALU.mult,
                                       ALU.subtract).then_inc(S["neg"], 1)

            def attend(G, g, b, first):
                dve.wait_ge(S["pvt"], G + 1)
                v.reciprocal(rec[:], A4[:, :, :, DH]).then_inc(S["rec_s"], 1)
                dve.wait_ge(S["rec_s"], G + 1)
                if not first and g == 0:
                    dve.wait_ge(S["attnT_ps"], 2 * b)
                v.tensor_tensor(attn[:, :, 64 * g:64 * g + 64].rearrange("p q (j d) -> p q j d", j=4),
                                A4[:, :, :, 0:DH], rec[:].rearrange("p q (j a) -> p q j a", a=1)
                                .to_broadcast([P, TT, 4, DH]), ALU.mult).then_inc(S["attn_g"], 1)

            def add_residual(t, h, first, m=2):
                dve.wait_ge(S["o_ps"], 2 * t + h + 1)
                dve.wait_ge(S["xb"], t + 1)
                if not first and h == 0:
                    dve.wait_ge(S["x1_st"], 16 * t)
                v.tensor_tensor(x1[:, 2 * h:2 * h + 2], rows_of(m), xr[:, 2 * h:2 * h + 2], ALU.add).then_inc(S["x1_s"], 1)

            def bc(a):
                return a.rearrange("p (t a) -> p t a", a=1).to_broadcast([P, TT, E])

            def route(t, step):
                if step:
                    dve.wait_ge(S["rtc"], RT * t + step)
                if step == 0:
                    dve.wait_ge(S["lg_ps"], t + 1)
                    i_ = v.tensor_copy(lg[:], M[0][:, 0:TT * E].rearrange("p (t e) -> p t e", e=E))
                if step == 1:
                    i_ = v.tensor_reduce(sm[:, 0], lg[:], AX.X, ALU.max)
                if step == 2:
                    i_ = v.tensor_tensor(rt[:, 0], lg[:], bc(sm[:, 0]), ALU.subtract)
                if step == 3:
                    i_ = v.tensor_scalar(rt[:, 2], rt[:, 0], 0.0, float(E), ALU.is_lt, ALU.mult)
                if step == 4:
                    i_ = v.tensor_tensor(rt[:, 3], rt[:, 2], iota_e[:], ALU.add)
                if step == 5:
                    i_ = v.tensor_reduce(sm[:, 1], rt[:, 3], AX.X, ALU.min)
                if step == 6:
                    i_ = v.tensor_tensor(rt[:, 4], iota_e[:], bc(sm[:, 1]), ALU.is_equal)
                if step == 7:
                    i_ = v.scalar_tensor_tensor(rt[:, 5], rt[:, 4], -1e30, lg[:], ALU.mult, ALU.add)
                if step == 8:
                    i_ = v.tensor_reduce(sm[:, 2], rt[:, 5], AX.X, ALU.max)
                if step == 9:
                    i_ = v.tensor_tensor(rt[:, 6], rt[:, 5], bc(sm[:, 2]), ALU.subtract)
                if step == 10:
                    i_ = v.tensor_scalar(rt[:, 7], rt[:, 6], 0.0, float(E), ALU.is_lt, ALU.mult)
                if step == 11:
                    i_ = v.tensor_tensor(rt[:, 8], rt[:, 7], iota_e[:], ALU.add)
                if step == 12:
                    i_ = v.tensor_reduce(sm[:, 3], rt[:, 8], AX.X, ALU.min)
                if step == 13:
                    i_ = v.tensor_tensor(rt[:, 9], iota_e[:], bc(sm[:, 3]), ALU.is_equal)
                if step == 14:
                    i_ = v.tensor_tensor(mask[:], rt[:, 4], rt[:, 9], ALU.add)
                i_.then_inc(S["rtc"], 1)

            def weigh(t, step, first):
                if step:
                    dve.wait_ge(S["wgt"], (WT - 1) * t + step)
                if step == 0:
                    dve.wait_ge(S["ex"], t + 1)
                    i_ = v.tensor_reduce(sm[:, 4], rt[:, 1], AX.X, ALU.add)
                if step == 1:
                    i_ = v.reciprocal(sm[:, 5], sm[:, 4])
                if step == 2:
                    i_ = v.tensor_tensor(rt[:, 10], rt[:, 1], rt[:, 9], ALU.mult)
                if step == 3:
                    i_ = v.tensor_reduce(sm[:, 6], rt[:, 10], AX.X, ALU.add)
                if step == 4:
                    i_ = v.tensor_tensor(sm[:, 7], sm[:, 6], sm[:, 5], ALU.mult)
                if step == 5:
                    i_ = v.scalar_tensor_tensor(sm[:, 8], sm[:, 5], 1e-9, sm[:, 7], ALU.add, ALU.add)
                if step == 6:
                    i_ = v.reciprocal(sm[:, 9], sm[:, 8])
                if step == 7:
                    i_ = v.tensor_tensor(sm[:, 10], sm[:, 5], sm[:, 9], ALU.mult)
                if step == 8:
                    i_ = v.tensor_tensor(sm[:, 11], sm[:, 7], sm[:, 9], ALU.mult)
                if step == 9:
                    i_ = v.tensor_tensor(rt[:, 11], rt[:, 4], bc(sm[:, 10]), ALU.mult)
                if step == 10:
                    i_ = v.tensor_tensor(rt[:, 12], rt[:, 9], bc(sm[:, 11]), ALU.mult)
                if step == 11:
                    if not first:
                        dve.wait_ge(S["sct"], 128 * t)
                    v.tensor_tensor(row[:, :, W_CW:W_CW + E], rt[:, 11], rt[:, 12], ALU.add).then_inc(S["cw_s"], 1)
                    return
                i_.then_inc(S["wgt"], 1)

            def place(t, step, first):
                if not (first and step == 0):
                    dve.wait_ge(S["plc"], (PT - 1) * t + min(step, PT - 2))
                C = M[0][:, 0:TT * E].rearrange("p (t e) -> p t e", e=E)
                if step == 0:
                    dve.wait_ge(S["rank_ps"], t + 1)
                    i_ = v.tensor_tensor(rt[:, 10], C, base[:, 0:1].to_broadcast([P, TT, E]), ALU.add)
                if step == 1:
                    i_ = v.tensor_tensor(base[:, 0], M[0][:, TT * E:TT * E + E], base[:, 0], ALU.add)
                if step == 2:
                    i_ = v.tensor_tensor(rt[:, 11], rt[:, 10], region[:], ALU.add)
                if step == 3:
                    i_ = v.tensor_tensor(rt[:, 12], rt[:, 11], rt[:, 4], ALU.mult)
                if step == 4:
                    i_ = v.tensor_tensor(rt[:, 13], rt[:, 11], rt[:, 9], ALU.mult)
                if step == 5:
                    i_ = v.tensor_reduce(slots[:], rt[:, 12:14].rearrange("p a t e -> p (a t) e"), AX.X, ALU.add)
                if step == 6:
                    if not first:
                        dve.wait_ge(S["sct"], 128 * t)
                    v.tensor_copy(slots_u[:], slots[:]).then_inc(S["slot"], 1)
                    return
                if step == 7:
                    i_ = v.tensor_copy(base[:, 1], base[:, 0])
                i_.then_inc(S["plc"], 1)

            def batch(b, first, last):
                n, t = b + 1, b - 1
                second = isinstance(b, int) and b == 1

                def middle(s):
                    if s % 4 == 2 and not (last and s == 14):
                        negate(4 * b + s // 4 + 1)
                    if s == 2 and not first:
                        attend(4 * b - 1, 3, t, False)
                    if s in (6, 11, 14):
                        attend(4 * b + s // 4 - 1, s // 4 - 1, b, first)

                def small(s, j):
                    if not first:
                        for k in range(*ROUTE_AT.get((s, j), (0, 0))):
                            route(t, k)
                        for k in range(*WEIGH_AT.get((s, j), (0, 0))):
                            weigh(t, k, second)
                        for k in range(*PLACE_AT.get((s, j), (0, 0))):
                            place(t, k, second)

                def begin(s):
                    if s in REST_STEPS and not last:
                        part_rest(n, ORDER[REST_STEPS.index(s)], False)
                    if s in (5, 6) and not first:
                        add_residual(t, s - 5, second)

                def end(s):
                    if s in (0, 1) and not last:
                        for tt in range(2):
                            stats_of(xt, n, 0, 2 * s + tt, (S["x_in"], 16 * (n + 1)))
                    if s == 1 and not last:
                        aggregate(n, 0)
                    if s == 3 and not last:
                        for k in range(4):
                            newton(n, 0, k)
                        normalise(xn, xt, n, 0, (S["xnT_ps"], 2 * n))
                    if s in (5, 6) and not first:
                        for tt in range(2):
                            stats_of(x1, t, 1, 2 * (s - 5) + tt, (S["x1_s"], 2 * t + s - 4))
                    if s == 6 and not first:
                        aggregate(t, 1)
                    if s == 7 and not first:
                        for k in range(4):
                            newton(t, 1, k)
                        normalise(xn2, x1, t, 1, None if second else (S["xl"], t))

                for s in range(STEPS):
                    for j in range(4):
                        if not last or s + LEAD < STEPS:
                            reduce(b, s + LEAD, j)
                        small(s, j)
                        if j == 0:
                            begin(s)
                        if j == 1:
                            middle(s)
                    end(s)
                    small(s, 4)

            v.memset(vaug[:], 1.0).then_inc(S["ones_s"], 1)

            for tt in range(TT):
                stats_of(xt, 0, 0, tt, (S["x_in"], 16))
            aggregate(0, 0)
            for k in range(4):
                newton(0, 0, k)
            normalise(xn, xt, 0, 0, None)
            dve.wait_ge(S["cin_k"], 16 * 3)
            for i, m in zip(ORDER, (2, 0, 2, 0)):
                if i == ORDER[2]:
                    dve.wait_ge(S["consts"], 1)
                part_rest(0, i, True, m)
            dve.wait_ge(S["ponce"], 14)
            for h in range(LEAD):
                for j in range(4):
                    reduce(0, h, j)
                if h == 3:
                    negate(0)

            batch(0, True, False)
            batch(1, False, False)
            with dve.Fori(2, B - 1) as b:
                batch(b, False, False)
            batch(B - 1, False, True)
            t = B - 1
            attend(4 * B - 1, 3, t, False)
            for h in range(2):
                add_residual(t, h, False, (2, 0)[h])
                for j in range(2):
                    stats_of(x1, t, 1, 2 * h + j, (S["x1_s"], 2 * t + h + 1))
            aggregate(t, 1)
            for k in range(4):
                newton(t, 1, k)
            normalise(xn2, x1, t, 1, (S["xl"], t))
            for k in range(RT):
                route(t, k)
            for k in range(WT):
                weigh(t, k, False)
            for k in range(PT):
                place(t, k, False)

            kf = 0

            def link(i_):
                nonlocal kf
                kf += 1
                i_.then_inc(S["fin"], 1)
                dve.wait_ge(S["fin"], kf)

            dve.wait_ge(S["plc"], (PT - 1) * B)
            link(v.tensor_copy(cnt_i[:, 0], base[:, 1]))
            link(v.tensor_scalar(cnt_f[:, 0], base[:, 1], float(P - 1), float(P), ALU.add, ALU.max))
            link(v.tensor_copy(cnt_i[:, 1], cnt_f[:, 0]))
            link(v.tensor_scalar(cnt_i[:, 2], cnt_i[:, 1], 7, None, ALU.logical_shift_right))
            link(v.tensor_copy(cnt_f[:, 1], cnt_i[:, 2]))
            link(v.memset(cnt_f[:, 0], 1.0))
            link(v.tensor_tensor_scan(cnt_f[:, 2], cnt_f[:, 0], cnt_f[:, 1], 0.0, ALU.mult, ALU.add))
            link(v.memset(tab[:, 0, 0:1], 0))
            link(v.tensor_copy(tab[:, 0, 1:E + 1], cnt_f[:, 2]))
            v.tensor_copy(tab[:, 1, 0:E], cnt_i[:, 0]).then_inc(S["tabs"], 1)

            def over_tiles(a):
                return a.rearrange("p (a e) -> p a e", a=1).to_broadcast([P, TN, E - 1])

            dve.wait_ge(S["w_l"], 2 * E)
            link(v.tensor_tensor(tt_f[:, 0], iota_t[:].rearrange("p (t a) -> p t a", a=1)
                                 .to_broadcast([P, TN, E - 1]), over_tiles(cnt_f[:, 2, 0:E - 1]), ALU.is_ge))
            link(v.tensor_tensor(tt_f[:, 1], tt_f[:, 0], over_tiles(cnt_f[:, 1, 0:E - 1]), ALU.mult))
            link(v.tensor_reduce(tt_s[:, 0:2], tt_f, AX.X, ALU.add))
            link(v.tensor_tensor(tt_s[:, 2], iota_t[:], tt_s[:, 1], ALU.subtract))
            link(v.tensor_scalar(tt_s[:, 3], tt_s[:, 2], float(P), None, ALU.mult))
            link(v.tensor_scalar(tt_s[:, 4], tt_s[:, 0], float(REGION), None, ALU.mult))
            link(v.tensor_tensor(tt_s[:, 5], tt_s[:, 3], tt_s[:, 4], ALU.add))
            link(v.scalar_tensor_tensor(tt_s[:, 6], iota_t[:], cnt_f[:, 2, E - 1:E], tt_s[:, 5],
                                        ALU.is_lt, ALU.mult))
            link(v.tensor_copy(tile_tab[:, 0], tt_s[:, 6]))
            v.tensor_copy(tile_tab[:, 1], tt_s[:, 0]).then_inc(S["tabs"], 1)

            dve.wait_ge(S["qk_ps"], 4 * B)
            v.memset(xT[:], 0.0).then_inc(S["xT_s"], 1)
            v.memset(hh, 0.0).then_inc(S["hh_s"], 2)
            v.memset(hl, 0.0).then_inc(S["hl_s"], 2)
            v.memset(ys, 0.0).then_inc(S["y_s"], 2)
            dve.wait_ge(S["xT_s"], 1)
            dve.wait_ge(S["hh_s"], 2)
            dve.wait_ge(S["hl_s"], 2)
            dve.wait_ge(S["tabs"], 1)
            last = dve.value_load(tab[0:1, 0, E:E + 1], min_val=8, max_val=MAXT)

            def xT_copy(i):
                dve.wait_ge(S["t_ps"], i + 1)
                v.tensor_copy(xT[:], XT16).then_inc(S["xT_s"], 1)

            def h_split(i, wait_s2):
                for k in range(2):
                    c = slice(T * k, T * k + T)
                    dve.wait_ge(S["gelu"], 2 * i + k + 3)
                    if wait_s2:
                        dve.wait_ge(S["s2"], i)
                    v.tensor_copy(hh[:, c], hf[:, c]).then_inc(S["hh_s"], 1)
                    dve.wait_ge(S["hh_s"], 2 * i + k + 3)
                    v.tensor_tensor(hl[:, c], hf[:, c], hh[:, c], ALU.subtract).then_inc(S["hl_s"], 1)

            def y_scale(i):
                dve.wait_ge(S["s2"], i + 1)
                dve.wait_ge(S["meta"], 32 * i + 32)
                dve.wait_ge(S["scat"], 16 * i + 16)
                v.tensor_copy(meta_id[:], meta_in[:]).then_inc(S["y_s"], 1)
                v.tensor_scalar(ys, PV[:, 0:D], meta_cw[:, 0:1], 1.0 / WSC, ALU.mult,
                                ALU.mult).then_inc(S["y_s"], 1)

            xT_copy(0)
            xT_copy(1)
            h_split(0, False)
            with dve.Fori(1, last) as i:
                xT_copy(i + 1)
                y_scale(i - 1)
                h_split(i, True)
            y_scale(last - 1)

        @block.tensor
        def _(pe):
            mm, tr = nc.tensor.matmul, nc.tensor.transpose
            pe.wait_ge(S["cin_k"], 16 * 3)

            def xnT_piece(n, c, after):
                pe.wait_ge(*after)
                pe.wait_ge(S["xn_s"], TT * (n + 1))
                for tt in range(TT):
                    i_ = tr(M[1][:, P * tt:P * tt + P], xn[:, tt, P * c:P * c + P], ident[:])
                i_.then_inc(S["xnT_ps"], 1)

            def qk_piece(n, i, after, m=2):
                if after is not None:
                    pe.wait_ge(*after)
                if i >= 2:
                    pe.wait_ge(S["ct_in"], 16 * (n + 1))
                else:
                    pe.wait_ge(S["xnT_sb"], 2 * n + 2)
                w, src = ((wq, xnT), (wk, ct))[i // 2]
                h = i % 2
                for c in range(KC):
                    i_ = mm(M[m][:], w[:, c, P * h:P * h + P], src[:, c, :], start=(c == 0), stop=(c == KC - 1))
                i_.then_inc(S["qk_ps"], 1)

            def v_piece(n, h, after, m=2):
                pe.wait_ge(*after)
                for q in range(2):
                    t_ = 2 * h + q
                    for c in range(KC):
                        i_ = mm(rows_of(m)[:, q], ct[:, c, P * t_:P * t_ + P], wv[:, c, :], start=(c == 0), stop=(c == KC - 1))
                i_.then_inc(S["v_ps"], 1)

            def max_piece(G, par, after):
                pe.wait_ge(*after)
                pe.wait_ge(S["red"], 16 * G + 16)
                tr(M[0][0:16, 0:P], mx[:, par].rearrange("p h t -> p (h t)"), ident[:]).then_inc(S["maxT"], 1)

            def pvt_piece(G, after):
                pe.wait_ge(*after)
                pe.wait_ge(S["pve"], G + 1)
                for q in range(TT):
                    i_ = tr(M[1][:, P * q:P * q + P], pvs[:, P * q:P * q + P], ident[:])
                i_.then_inc(S["pvt"], 1)

            def attnT_piece(t, c, after):
                pe.wait_ge(*after)
                pe.wait_ge(S["attn_g"], 4 * (t + 1))
                for tt in range(TT):
                    i_ = tr(M[1][:, P * tt:P * tt + P], attn[:, tt, P * c:P * c + P], ident[:])
                i_.then_inc(S["attnT_ps"], 1)

            def o_piece(t, h, after, m=2):
                pe.wait_ge(*after)
                pe.wait_ge(S["attnT_sb"], 2 * t + 2)
                for q in range(2):
                    t_ = 2 * h + q
                    for c in range(KC):
                        i_ = mm(rows_of(m)[:, q], attnT[:, c, P * t_:P * t_ + P], wo[:, c, :], start=(c == 0), stop=(c == KC - 1))
                i_.then_inc(S["o_ps"], 1)

            def xn2T_piece(t, c, after):
                pe.wait_ge(*after)
                pe.wait_ge(S["xn2_s"], TT * (t + 1))
                for tt in range(TT):
                    i_ = tr(M[1][:, P * tt:P * tt + P], xn2[:, tt, P * c:P * c + P], ident[:])
                i_.then_inc(S["xn2T_ps"], 1)

            def lgT_piece(t, after):
                pe.wait_ge(*after)
                pe.wait_ge(S["xn2T_sb"], 2 * t + 2)
                for c in range(KC):
                    i_ = mm(M[2][0:E, :], rw[:, c, :], xn2T[:, c, :], start=(c == 0), stop=(c == KC - 1))
                i_.then_inc(S["lgT_ps"], 1)

            def lg_piece(t, after):
                wait(pe, *after)
                wait(pe, S["lgT_sb"], t + 1)
                for tt in range(TT):
                    i_ = tr(M[0][:, E * tt:E * tt + E], lgT[:, P * tt:P * tt + P], ident[0:E, 0:E])
                i_.then_inc(S["lg_ps"], 1)

            def rank_piece(t, after=None):
                if after is not None:
                    pe.wait_ge(*after)
                pe.wait_ge(S["rtc"], RT * (t + 1))
                mk = mask[:].rearrange("p t e -> p (t e)")
                mm(M[0][:, 0:TT * E], tri[:], mk, start=True, stop=False, skip_group_check=True)
                for k in range(1, TT):
                    mm(M[0][:, k * E:TT * E], ones[:], mk[:, 0:(TT - k) * E], start=False, stop=False, skip_group_check=True)
                for k in range(TT):
                    i_ = mm(M[0][:, TT * E:TT * E + E], ones[:], mk[:, k * E:k * E + E], start=False,
                            stop=(k == TT - 1), skip_group_check=True)
                i_.then_inc(S["rank_ps"], 1)

            def score_a(b, h, j):
                g = (h // 4) % 4
                if j == 0 and h % 4 == 0:
                    pe.wait_ge(qk_in[g], 96 * (b + 1 + h // 16))
                if not (isinstance(b, int) and b == 0 and h == 0 and j < 2):
                    pe.wait_ge(S["red"], (16 * b + h) * 4 + j - 1)
                mm(A[:, j % 2, :], qst[0:KS, g, h % 4, P * j:P * j + P], kst[0:KS, g, h % 4, :],
                   start=True, stop=True).then_inc(S["a_done"], 1)

            def score_b(b, s, j, first):
                g, kc = s // 4, s % 4
                if kc == 0 and j == 0:
                    pe.wait_ge(mrow[g], 32 * (b + 1))
                if not (first and s == 0 and j < 2):
                    pe.wait_ge(S["exp"], (16 * b + s) * 4 + j - 1)
                mm(Bp[:, j % 2, :], kst[0:KM, g, j, P * kc:P * kc + P], qst[0:KM, g, j, :],
                   start=True, stop=True).then_inc(S["b_done"], 1)

            def values(b, s, first):
                g, kc = (s // 4) % 4, s % 4
                pe.wait_ge(S["exp"], (16 * b + s) * 4 + 4)
                if kc == 0:
                    pe.wait_ge(S["vaug_s"], 4 * b + g + 1)
                    if not (first and s == 0):
                        pe.wait_ge(S["pve"], 4 * b + g)
                for j in range(4):
                    i_ = mm(PV[32 * j:32 * j + 32, :], vaug[:, g, kc, j, :], pT[:, s % 2, j, :],
                            start=(kc == 0), stop=(kc == 3))
                i_.then_inc(S["pv"], 1)

            def batch(b, first, last):
                n, t = b + 1, b - 1
                second = isinstance(b, int) and b == 1

                def middle(s):
                    if s % 4 == 2 and not (last and s == 14):
                        G = 4 * b + s // 4 + 1
                        after = (S["neg"], 2 * G)
                        if s == 2 and not (first or second):
                            after = (S["slot"], b - 1)
                        if s == 14 and not first:
                            after = (S["rtc"], RT * t + 1)
                        max_piece(G, (s // 4 + 1) % 2, after)
                    if s == 2 and not first:
                        pvt_piece(4 * b - 1, (S["attn_g"], 4 * b - 1))
                    if s == 3 and not first:
                        attnT_piece(t, 0, (S["attn_g"], 4 * b))
                    if s == 4 and not last:
                        xnT_piece(n, 0, (S["xnT_sb"], 2) if first else (S["attnT_sb"], 2 * t + 2))
                    if s == 5 and not last:
                        xnT_piece(n, 1, (S["xnT_sb"], 2 * n + 1))
                    if s == 6:
                        pvt_piece(4 * b, (S["attnT_sb"], 2 * t + 2) if last else (S["xnT_sb"], 2 * n + 2))
                    if s == 9 and not first:
                        xn2T_piece(t, 0, (S["attn_g"], 4 * b + 1))
                    if s == 10 and not first:
                        lgT_piece(t, (S["x1_s"], 2 * t + 2) if last else (S["r_s"], 4 * n + 4))
                    if s == 11:
                        pvt_piece(4 * b + 1, (S["attn_g"], 4 * b + 1) if first else (S["xn2T_sb"], 2 * t + 2))
                    if s == 14:
                        pvt_piece(4 * b + 2, (S["attn_g"], 4 * b + 2))

                def end(s):
                    if s in QK_STEPS and not last:
                        k = QK_STEPS.index(s)
                        after = ((S["v_sb"], 2 * b + 2), (S["r_s"], 4 * n + 1),
                                 (S["r_s"], 4 * n + 2) if first else (S["x1_s"], 2 * t + 2), (S["r_s"], 4 * n + 3))[k]
                        qk_piece(n, ORDER[k], after)
                    if s == 3 and not first:
                        attnT_piece(t, 1, (S["attnT_sb"], 2 * t + 1))
                    if s == 4 and not first:
                        o_piece(t, 0, (S["v_sb"], 2 * b + 2) if last else (S["r_s"], 4 * n + 2))
                    if s == 5 and not first:
                        o_piece(t, 1, (S["x1_s"], 2 * t + 1))
                    if s == 9 and not first:
                        xn2T_piece(t, 1, (S["xn2T_sb"], 2 * t + 1))
                    if s == 10 and not first:
                        lg_piece(t, (S["neg"], 2 * (4 * b + 3) + 2))
                    if s == 14 and not last:
                        v_piece(n, 0, (S["r_s"], 4 * n + 4) if first else (S["lgT_sb"], t + 1))
                    if s == 14 and not first:
                        rank_piece(t, None if last else (S["neg"], 2 * (4 * b + 4) + 2))
                    if s == 15 and not last:
                        v_piece(n, 1, (S["v_sb"], 2 * n + 1))

                for s in range(STEPS):
                    for j in range(4):
                        if not last or s + LEAD < STEPS:
                            score_a(b, s + LEAD, j)
                        score_b(b, s, j, first)
                        if j == 1:
                            middle(s)
                            if not (first and s == 0):
                                values(b, s - 1, first)
                    end(s)

            qk_piece(0, 2, None, 2)
            pe.wait_ge(S["ponce"], 6)
            for c in range(KC):
                xnT_piece(0, c, (S["xn_s"], TT) if c == 0 else (S["xnT_sb"], 1))
            qk_piece(0, 3, None, 0)
            pe.wait_ge(S["consts"], 1)
            qk_piece(0, 0, (S["r_s"], 1), 2)
            qk_piece(0, 1, (S["r_s"], 2), 0)
            pe.wait_ge(S["cin"], 16 * 5)
            v_piece(0, 0, (S["r_s"], 3), 2)
            v_piece(0, 1, (S["r_s"], 4), 0)
            pe.wait_ge(S["ones_s"], 1)
            for h in range(LEAD):
                for j in range(4):
                    score_a(0, h, j)
                if h == 3:
                    max_piece(0, 0, (S["v_sb"], 2))

            pe.wait_ge(S["kst_ones"], 4)
            batch(0, True, False)
            batch(1, False, False)
            with pe.Fori(2, B - 1) as b:
                batch(b, False, False)
            batch(B - 1, False, True)
            t = B - 1
            values(B, -1, False)
            pvt_piece(4 * B - 1, (S["attn_g"], 4 * B - 1))
            attnT_piece(t, 0, (S["attn_g"], 4 * B))
            attnT_piece(t, 1, (S["attnT_sb"], 2 * t + 1))
            o_piece(t, 0, (S["lgT_sb"], t))
            o_piece(t, 1, (S["slot"], t), 0)
            xn2T_piece(t, 0, (S["attnT_sb"], 2 * t + 2))
            xn2T_piece(t, 1, (S["xn2T_sb"], 2 * t + 1))
            lgT_piece(t, (S["x1_s"], 2 * t + 1))
            lg_piece(t, (S["x1_s"], 2 * t + 2))
            rank_piece(t)

            def turn(i):
                pe.wait_ge(S["xrow_s"], i + 1)
                pe.wait_ge(S["xT_s"], i + 1)
                for c in range(4):
                    i_ = tr(XT16[:, P * c:P * c + P], xrow16[:, P * c:P * c + P], ident16[:])
                i_.then_inc(S["t_ps"], 1)

            def up(i, q):
                pe.wait_ge(S["xT_s"], i + 2)
                for k in range(2):
                    pe.wait_ge(S["gelu"], 2 * i + k + 1)
                    for m in range(4):
                        hc = 4 * k + m
                        terms = [(wp, c, xp) for c in range(KC) for wp, xp in ((0, 0), (0, 1), (1, 0))]
                        for z, (wp, c, xp) in enumerate(terms):
                            i_ = mm(A[:, k, P * m:P * m + P],
                                    whl[q][:, (2 * wp + c) * HID + P * hc:(2 * wp + c) * HID + P * hc + P],
                                    xT[:, (2 * xp + c) * P:(2 * xp + c) * P + P], start=(z == 0), stop=(z == 5))
                    i_.then_inc(S["s1"], 1)

            def down(i, q):
                pe.wait_ge(S["y_s"], 2 * i + 2)
                for k in range(2):
                    pe.wait_ge(S["hl_s"], 2 * i + k + 3)
                    for m in range(4):
                        hc = 4 * k + m
                        for z, (hp, wp) in enumerate(((hh, 0), (hh, 1), (hl, 0))):
                            at = (4 + 2 * wp) * HID + D * hc
                            i_ = mm(PV[:, 0:D], hp[:, P * hc:P * hc + P], whl[q][:, at:at + D],
                                    start=(hc == 0 and z == 0), stop=(hc == HC - 1 and z == 2))
                i_.then_inc(S["s2"], 1)

            pe.wait_ge(S["tabs"], 1)
            pe.wait_ge(S["pve"], 4 * B)
            pe.wait_ge(S["xn2T_sb"], 2 * B)
            pe.wait_ge(S["red"], 64 * B)

            def expert(pair, q, first):
                e = 2 * pair + q
                lo = pe.value_load(tab[0:1, 0, bass.ds(e, 1)], min_val=0, max_val=MAXT - 1)
                hi = pe.value_load(tab[0:1, 0, bass.ds(e + 1, 1)], min_val=1, max_val=MAXT)
                pe.wait_ge(wld[q], 16 * (pair + 1))
                up(lo, q)
                turn(lo + 1)
                if not first:
                    down(lo - 1, 1 - q)
                with pe.If(lo + 1 < hi):
                    with pe.Fori(lo + 1, hi) as i:
                        up(i, q)
                        turn(i + 1)
                        down(i - 1, q)
                with pe.Else():
                    pass

            turn(0)
            expert(0, 0, True)
            expert(0, 1, False)
            with pe.Fori(1, E // 2) as pair:
                expert(pair, 0, False)
                expert(pair, 1, False)
            last = pe.value_load(tab[0:1, 0, E:E + 1], min_val=8, max_val=MAXT)
            down(last - 1, 1)


RT = 15
WT = 12
PT = 8
ROUTE_AT = {(11, 0): (0, 1), (11, 1): (1, 2), (11, 2): (2, 3), (11, 3): (3, 4), (12, 0): (4, 5), (12, 1): (5, 6),
            (12, 2): (6, 7), (12, 3): (7, 9), (13, 0): (9, 11), (13, 1): (11, 12), (13, 2): (12, 14), (13, 3): (14, 15)}
WEIGH_AT = {(14, 0): (0, 1), (14, 1): (1, 2), (14, 2): (2, 3), (14, 3): (3, 4), (14, 4): (4, 9), (15, 0): (9, 10),
            (15, 1): (10, 11), (15, 2): (11, 12)}
PLACE_AT = {(15, 4): (0, 8)}

_INS = ["x", "ctxT", "wqT", "wkT", "wvT", "woT", "bq", "bk", "bv", "bo", "rwT", "w1", "w2"]


def kernel(x, ctx_1024, L0_xattn_wq_w, L0_xattn_wq_b, L0_xattn_wk_w, L0_xattn_wk_b, L0_xattn_wv_w, L0_xattn_wv_b,
           L0_xattn_wo_w, L0_xattn_wo_b, L0_ffn_router_w, L0_ffn_w1, L0_ffn_w2):
    import numpy as np
    import concourse.bacc as bacc
    from concourse.bass_utils import run_bass_kernel_spmd

    arrays = {
        "x": x, "ctxT": np.transpose(np.asarray(ctx_1024), (0, 2, 1)),
        "wqT": np.asarray(L0_xattn_wq_w).T, "wkT": np.asarray(L0_xattn_wk_w).T,
        "wvT": np.asarray(L0_xattn_wv_w).T, "woT": np.asarray(L0_xattn_wo_w).T,
        "bq": L0_xattn_wq_b, "bk": L0_xattn_wk_b, "bv": L0_xattn_wv_b, "bo": L0_xattn_wo_b,
        "rwT": np.asarray(L0_ffn_router_w).T, "w1": L0_ffn_w1, "w2": L0_ffn_w2,
    }
    nc = bacc.Bacc("TRN2", target_bir_lowering=False, num_devices=1)
    ins, args = {}, []
    for name in _INS:
        a = np.ascontiguousarray(arrays[name])
        ins[f"in_{name}"] = a
        args.append(nc.dram_tensor(f"in_{name}", a.shape, mybir.dt.from_np(a.dtype), kind="ExternalInput").ap())
    out = nc.dram_tensor("out_rows", (N + P, D), F32, kind="ExternalOutput").ap()
    build(nc, *args, out)
    r = run_bass_kernel_spmd(nc, [ins], core_ids=[0])
    return r.results[0]["out_rows"][0:N].reshape(B, T, D)
```
